# Optimizing a Trainium2 kernel written in Bass

```python
import numpy as np
import jax
import jax.numpy as jnp

def _softmax(x, axis=-1):
    return jax.nn.softmax(x, axis=axis)

def _gelu(x):
    return jax.nn.gelu(x, approximate=True)

def _silu(x):
    return jax.nn.silu(x)

def _sigmoid(x):
    return jax.nn.sigmoid(x)

def _layernorm(x, axis=-1, eps=1e-05):
    m = jnp.mean(x, axis=axis, keepdims=True)
    v = jnp.var(x, axis=axis, keepdims=True)
    return (x - m) / jnp.sqrt(v + eps)

def _scatter_add(tgt, idx, src, axis=0):
    return tgt.at[idx].add(src)

def _segment_sum(src, seg, n):
    return jax.ops.segment_sum(src, seg, n)
kernel_name = 'mk_seq_preln_d1_jaxref_r8_e4fd31'

def setup_inputs(seed: int=0):
    np.random.seed(seed)
    _w = jnp.asarray

    def _L0_attn_setup():
        import jax, jax.numpy as jnp
        import numpy as np
        HIDDEN = 256
        NUM_HEADS = 16
        HEAD_DIM = 128
        WINDOW = 128
        ROPE_THETA = 10000.0
        B, L = (1, 512)

        def _apply_rotary(x, cos, sin):
            d2 = x.shape[-1] // 2
            x1, x2 = (x[..., :d2], x[..., d2:])
            return jnp.concatenate([x1 * cos - x2 * sin, x2 * cos + x1 * sin], axis=-1)
        key = jax.random.key(seed)
        k0, k1, k2, k3, k4 = jax.random.split(key, 5)
        s = 1.0 / np.sqrt(HIDDEN)
        return {'hidden_states': jax.random.normal(k0, (B, L, HIDDEN), dtype=jnp.float32), 'wq': jax.random.normal(k1, (HIDDEN, NUM_HEADS * HEAD_DIM), dtype=jnp.float32) * s, 'wk': jax.random.normal(k2, (HIDDEN, NUM_HEADS * HEAD_DIM), dtype=jnp.float32) * s, 'wv': jax.random.normal(k3, (HIDDEN, NUM_HEADS * HEAD_DIM), dtype=jnp.float32) * s, 'wo': jax.random.normal(k4, (NUM_HEADS * HEAD_DIM, HIDDEN), dtype=jnp.float32) * s}
    _L0_attn_in = _L0_attn_setup()

    def _L0_ffn_setup():
        import jax, jax.numpy as jnp
        import numpy as np
        EPS = 1e-08

        def _bit_quant(w):
            scale = jnp.maximum(jnp.mean(jnp.abs(w)), EPS)
            w_ternary = jnp.clip(jnp.round(w / scale), -1.0, 1.0)
            return w + jax.lax.stop_gradient(w_ternary - w)
        key = jax.random.key(seed)
        k = jax.random.split(key, 5)
        emb, dff = (256, 1024)
        B, S = (4, 256)
        x = jax.random.normal(k[0], (B, S, emb), dtype=jnp.float32)
        w1 = jax.random.normal(k[1], (dff, emb), dtype=jnp.float32) * 0.02
        b1 = jax.random.normal(k[2], (dff,), dtype=jnp.float32) * 0.02
        w2 = jax.random.normal(k[3], (emb, dff), dtype=jnp.float32) * 0.02
        b2 = jax.random.normal(k[4], (emb,), dtype=jnp.float32) * 0.02
        return {'x': x, 'w1': w1, 'b1': b1, 'w2': w2, 'b2': b2}
    _L0_ffn_in = _L0_ffn_setup()
    _d = {'L0_attn_hidden_states': _L0_attn_in['hidden_states'], 'L0_attn_wq': _L0_attn_in['wq'], 'L0_attn_wk': _L0_attn_in['wk'], 'L0_attn_wv': _L0_attn_in['wv'], 'L0_attn_wo': _L0_attn_in['wo'], 'L0_ffn_w1': _L0_ffn_in['w1'], 'L0_ffn_b1': _L0_ffn_in['b1'], 'L0_ffn_w2': _L0_ffn_in['w2'], 'L0_ffn_b2': _L0_ffn_in['b2']}
    _x0 = _d['L0_attn_hidden_states']
    _d['L0_attn_hidden_states'] = jax.random.normal(jax.random.fold_in(jax.random.key(seed), 1), (1, 1024, 256), dtype=_x0.dtype)
    del _x0
    return _d

def reference(L0_attn_hidden_states, L0_attn_wq, L0_attn_wk, L0_attn_wv, L0_attn_wo, L0_ffn_w1, L0_ffn_b1, L0_ffn_w2, L0_ffn_b2):

    def _L0_attn_ref(hidden_states, wq, wk, wv, wo):
        import jax, jax.numpy as jnp
        import numpy as np
        HIDDEN = 256
        NUM_HEADS = 16
        HEAD_DIM = 128
        WINDOW = 128
        ROPE_THETA = 10000.0
        B, L = (1, 512)

        def _apply_rotary(x, cos, sin):
            d2 = x.shape[-1] // 2
            x1, x2 = (x[..., :d2], x[..., d2:])
            return jnp.concatenate([x1 * cos - x2 * sin, x2 * cos + x1 * sin], axis=-1)
        Bsz, Ln, _ = hidden_states.shape
        dtype = hidden_states.dtype
        scale = HEAD_DIM ** (-0.5)

        def split_heads(x):
            return x.reshape(Bsz, Ln, NUM_HEADS, HEAD_DIM).transpose(0, 2, 1, 3)
        q = split_heads(hidden_states @ wq)
        k = split_heads(hidden_states @ wk)
        v = split_heads(hidden_states @ wv)
        inv_freq = 1.0 / ROPE_THETA ** (jnp.arange(0, HEAD_DIM, 2, dtype=jnp.float32) / HEAD_DIM)
        pos = jnp.arange(Ln, dtype=jnp.float32)
        freqs = pos[:, None] * inv_freq[None, :]
        cos = jnp.cos(freqs).astype(dtype)
        sin = jnp.sin(freqs).astype(dtype)
        q = _apply_rotary(q, cos, sin)
        k = _apply_rotary(k, cos, sin)
        q_pos = jnp.arange(Ln)[:, None]
        k_pos = jnp.arange(Ln)[None, :]
        valid = (k_pos > q_pos - WINDOW) & (k_pos <= q_pos)
        neg = jnp.finfo(dtype).min
        attn = jnp.einsum('bhqd,bhkd->bhqk', q, k) * scale
        attn = jnp.where(valid, attn, neg)
        attn = jax.nn.softmax(attn, axis=-1)
        out = jnp.einsum('bhqk,bhkd->bhqd', attn, v)
        out = out.transpose(0, 2, 1, 3).reshape(Bsz, Ln, NUM_HEADS * HEAD_DIM)
        return out @ wo

    def _L0_ffn_ref(x, w1, b1, w2, b2):
        import jax, jax.numpy as jnp
        import numpy as np
        EPS = 1e-08

        def _bit_quant(w):
            scale = jnp.maximum(jnp.mean(jnp.abs(w)), EPS)
            w_ternary = jnp.clip(jnp.round(w / scale), -1.0, 1.0)
            return w + jax.lax.stop_gradient(w_ternary - w)
        w1q = _bit_quant(w1)
        w2q = _bit_quant(w2)
        h = jnp.einsum('bsd,fd->bsf', x, w1q) + b1
        h = jax.nn.gelu(h, approximate=False)
        return jnp.einsum('bsf,df->bsd', h, w2q) + b2
    x = L0_attn_hidden_states
    x = x + _L0_attn_ref(_layernorm(x, axis=-1), L0_attn_wq, L0_attn_wk, L0_attn_wv, L0_attn_wo)
    x = x + _L0_ffn_ref(_layernorm(x, axis=-1), L0_ffn_w1, L0_ffn_b1, L0_ffn_w2, L0_ffn_b2)
    return x

_drawn_inputs = setup_inputs


def setup_inputs(seed=0):
    import zlib

    import numpy as np

    out = dict(_drawn_inputs(seed))
    spreads = {}
    factors = {'L0_ffn_b1': 42.62, 'L0_ffn_b2': 64.0}
    for name, (base, spread) in spreads.items():
        noise = np.random.default_rng([zlib.crc32(name.encode()), seed]).standard_normal(out[name].shape)
        drawn = base * np.exp(spread * noise) if base else spread * noise
        out[name] = jnp.asarray(drawn.astype(out[name].dtype))
    for name, factor in factors.items():
        out[name] = (out[name] * factor).astype(out[name].dtype)
    return out
```

```python
from contextlib import ExitStack

import concourse.bass as bass
from concourse import mybir

P = 128
ALU = mybir.AluOpType
ACT = mybir.ActivationFunctionType
AX = mybir.AxisListType
F32 = mybir.dt.float32
F32R = mybir.dt.float32r
BIG = 3.4028234663852886e38


def preln_block_kernel(nc, x, wq, wk, wv, wo, w1t, b1, w2t, b2, cos_t, sin_t, in_prev, mask_t, ident, out):
    T, D = x.shape
    HD = P
    HEADS = wq.shape[1] // HD
    PAIRS = HEADS // 2
    NT = T // P
    KD = D // P
    F = w1t.shape[1]
    NF = F // P
    HALF = T // 2
    SCALE = float(HD) ** -0.5
    EPS_LN = 1e-5
    EPS_Q = 1e-8
    NW = D * F
    CHUNKS = 4 * HEADS
    LAST = 8 * PAIRS - 1
    assert T == 1024 and D == 256 and F == 1024

    with ExitStack() as ctx:
        def sb(name, shape, dt=F32):
            return ctx.enter_context(nc.sbuf_tensor(name, shape, dt))

        def bank(name):
            return ctx.enter_context(nc.psum_tensor(name, [P, 512], F32))

        def sem(name):
            return ctx.enter_context(nc.semaphore(name))

        xres = sb("xres", [P, NT, D])
        xnorm = sb("xnorm", [P, NT, D])
        xT_hi = sb("xT_hi", [P, KD, T], F32R)
        xT_lo = sb("xT_lo", [P, KD, T], F32R)
        qk_raw = [sb(f"qk_raw{a}", [P, 2, KD, HD]) for a in range(2)]
        qk_hi = [sb(f"qk_hi{a}", [P, 2, KD, HD], F32R) for a in range(2)]
        qk_lo = [sb(f"qk_lo{a}", [P, 2, KD, HD], F32R) for a in range(2)]
        v_raw = sb("v_raw", [P, KD, 2 * HD])
        v_hi = sb("v_hi", [P, KD, 2 * HD], F32R)
        v_lo = sb("v_lo", [P, KD, 2 * HD], F32R)
        o_raw = sb("o_raw", [P, 2, D])
        o_hi = sb("o_hi", [P, 2, D], F32R)
        o_lo = sb("o_lo", [P, 2, D], F32R)
        turn = [sb(f"turn{c}", [P, 512]) for c in range(4)]
        swapped = [sb(f"swapped{c}", [P, 512]) for c in range(4)]
        cos_sb = sb("cos_sb", [P, T])
        sin_sb = sb("sin_sb", [P, T])
        in_prev_sb = sb("in_prev_sb", [P, P], mybir.dt.int32)
        mask_sb = sb("mask_sb", [P, 2, P])
        nothing = sb("nothing", [P, P])
        ident_sb = sb("ident_sb", [P, P])
        probs = [sb(f"probs{i}", [P, 2, P]) for i in range(2)]
        rowmax = sb("rowmax", [P, 2, 2])
        negmax = sb("negmax", [P, 2, 2])
        rowsum = sb("rowsum", [P, 2, 2])
        rinv = sb("rinv", [P, 2, 2])
        probsT = sb("probsT", [P, 2, 2, P])
        v_sb = sb("v_sb", [P, NT, 2 * HD])
        gT_hi = sb("gT_hi", [P, NF, T], F32R)
        gT_lo = sb("gT_lo", [P, NF, T], F32R)

        def rot_hi(a, w):
            return gT_hi[:, 2 * a + w]

        def rot_lo(a, w):
            return gT_lo[:, 2 * a + w]

        def oT_hi(a):
            return gT_hi[:, 4 + a]

        def oT_lo(a):
            return gT_lo[:, 4 + a]

        w1_raw = sb("w1_raw", [P, KD * F])
        w2_raw = sb("w2_raw", [P, NF * D])
        w1_sb = sb("w1_sb", [P, KD, F], F32R)
        w2_sb = sb("w2_sb", [P, NF, D], F32R)
        b1_sb = sb("b1_sb", [P, NF])
        b2_sb = sb("b2_sb", [P, D])
        stats = sb("stats", [P, NT, 6])
        mv = sb("mv", [P, NT, 2])
        rstd = sb("rstd", [P, NT])
        var_eps = sb("var_eps", [P, NT])
        minus_half = sb("minus_half", [P, NT])
        mean_ones = sb("mean_ones", [P, P])
        abs_sum = sb("abs_sum", [P, 2, 4])
        mean_abs = sb("mean_abs", [P, 2])
        thr = sb("thr", [P, 2, 2])
        gelu_tmp = turn
        final = xnorm

        PR = [bank(f"PR{i}") for i in range(2)]
        SC = [bank(f"SC{i}") for i in range(2)]
        PT = bank("PT")
        OT = bank("OT")
        VO = [bank(f"VO{i}") for i in range(2)]

        x_in = [sem(f"x_in{i}") for i in range(4)]
        tab_in = [sem(f"tab_in{i}") for i in range(2)]
        mask_in = sem("mask_in")
        ident_in = sem("ident_in")
        bias_in = sem("bias_in")
        w12_in = [sem(f"w{k + 1}_in") for k in range(2)]
        qk_in = [sem(f"qk_in{a}") for a in range(2)]
        v_in = sem("v_in")
        o_in = sem("o_in")
        swap_in = [sem(f"swap_in{c}") for c in range(4)]
        consts_set = sem("consts_set")
        nothing_set = sem("nothing_set")
        bn_done = sem("bn_done")
        aggr_done = sem("aggr_done")
        var_ready = sem("var_ready")
        rstd_ready = sem("rstd_ready")
        xn_ready = sem("xn_ready")
        xt_ready = sem("xt_ready")
        xt_hi_done = sem("xt_hi_done")
        xt_lo_done = sem("xt_lo_done")
        qkhi_done = sem("qkhi_done")
        qklo_done = sem("qklo_done")
        vhi_done = sem("vhi_done")
        vlo_done = sem("vlo_done")
        ohi_done = sem("ohi_done")
        olo_done = sem("olo_done")
        proj_done = sem("proj_done")
        proj_copied = sem("proj_copied")
        cos_done = sem("cos_done")
        sin_done = sem("sin_done")
        rot_done = sem("rot_done")
        rothi_done = sem("rothi_done")
        rotlo_done = sem("rotlo_done")
        scores_done = sem("scores_done")
        merged = sem("merged")
        max_done = sem("max_done")
        negmax_done = sem("negmax_done")
        exp_done = sem("exp_done")
        rinv_done = sem("rinv_done")
        scaled = sem("scaled")
        pt_done = sem("pt_done")
        pt_masked = sem("pt_masked")
        pv_done = sem("pv_done")
        othi_done = sem("othi_done")
        otlo_done = sem("otlo_done")
        v_done = sem("v_done")
        v_copied = sem("v_copied")
        wo_done = sem("wo_done")
        wo_added = sem("wo_added")
        abs_done = sem("abs_done")
        mean_done = sem("mean_done")
        mean_read = sem("mean_read")
        thr_done = sem("thr_done")
        below_done = [sem("w1_below"), sem("w2_below")]
        above_done = sem("w2_above")
        tern_done = [sem("w1_ternary"), sem("w2_ternary")]
        h_done = sem("h_done")
        gelu_done = sem("gelu_done")
        ghi_done = sem("ghi_done")
        glo_done = [sem("glo_dve"), sem("glo_pool")]
        b2_added = sem("b2_added")
        y_done = sem("y_done")
        fin_done = sem("fin_done")
        out_done = sem("out_done")

        def half_of(c):
            return slice((c // 2) * HALF, (c // 2 + 1) * HALF)

        def before(s, d=1):
            return ((s - d) % 8) // 4, (s - d) % 4

        def glo_count(k):
            return k // 4 + 1 if k % 4 == 3 else k - k // 4 + 1


        block = ctx.enter_context(nc.Block())

        @block.sync
        def _(sp):
            xv = x.rearrange("(t p) d -> p t d", p=P)
            ov = out.rearrange("(t p) d -> p t d", p=P)

            def load_head(head, a):
                for w, src in ((0, wq), (1, wk)):
                    s = src.rearrange("(k p) n -> p k n", p=P)
                    sp.dma_start(qk_raw[a][:, w], s[:, :, bass.ds(head * HD, HD)]).then_inc(qk_in[a], 16)

            def load_v(pair):
                s = wv.rearrange("(k p) n -> p k n", p=P)
                sp.dma_start(v_raw[:], s[:, :, bass.ds(pair * 2 * HD, 2 * HD)]).then_inc(v_in, 16)

            def load_o(pair):
                s = wo[bass.ds(pair * 2 * HD, 2 * HD), :].rearrange("(a p) n -> p a n", p=P)
                sp.dma_start(o_raw[:], s).then_inc(o_in, 16)

            def load_tables(half):
                hs = slice(half * HALF, (half + 1) * HALF)
                sp.dma_start(cos_sb[:, hs], cos_t[:, hs]).then_inc(tab_in[half], 16)
                sp.dma_start(sin_sb[:, hs], sin_t[:, hs]).then_inc(tab_in[half], 16)

            def swap(m, c):
                sp.wait_ge(proj_copied, m + 1)
                for to, fr in ((0, HD // 2), (HD // 2, 0)):
                    sp.dma_start(swapped[c][to:to + HD // 2, :],
                                 turn[c][fr:fr + HD // 2, :]).then_inc(swap_in[c], 16)

            def pair_steps(pair, ahead, first=False):
                for s in range(8):
                    if not (ahead == 0 and s >= 4):
                        swap(8 * pair + s + 4, s % 4)
                    if first and s in (1, 2):
                        h = NF // 2
                        fs = slice((s - 1) * h, s * h)
                        sp.dma_start(w2_raw[:].rearrange("p (f n) -> p f n", f=NF)[:, fs],
                                     w2t.rearrange("(f p) n -> p f n", p=P)[:, fs]).then_inc(w12_in[1], 16)
                    if s == 2 and ahead == 2:
                        sp.wait_ge(qklo_done, 2 * pair + 3)
                        load_head(2 * pair + 4, 0)
                    if s == 6 and ahead == 2:
                        sp.wait_ge(qklo_done, 2 * pair + 4)
                        load_head(2 * pair + 5, 1)
                    if s == 4 and ahead == 2:
                        sp.wait_ge(vlo_done, pair + 2)
                        load_v(pair + 2)
                    if s == 7 and ahead >= 1:
                        sp.wait_ge(olo_done, pair + 1)
                        load_o(pair + 1)

            for i in range(4):
                sp.dma_start(xres[:, 2 * i:2 * i + 2], xv[:, 2 * i:2 * i + 2]).then_inc(x_in[i], 16)
                if i == 0:
                    sp.dma_start(ident_sb[:], ident).then_inc(ident_in, 16)
                if i == 1:
                    load_head(0, 0)
            load_v(0)
            load_tables(0)
            load_head(1, 1)
            sp.dma_start(in_prev_sb[:], in_prev).then_inc(mask_in, 16)
            sp.dma_start(mask_sb[:].rearrange("p b q -> p (b q)"), mask_t).then_inc(mask_in, 16)
            load_tables(1)
            sp.wait_ge(qklo_done, 1)
            load_head(2, 0)
            swap(0, 0)
            swap(1, 1)
            sp.dma_start(w1_raw[:].rearrange("p (k f) -> p k f", k=KD),
                         w1t.rearrange("(k p) f -> p k f", p=P)).then_inc(w12_in[0], 16)
            sp.wait_ge(vlo_done, 1)
            load_v(1)
            load_o(0)
            swap(2, 2)
            swap(3, 3)
            sp.wait_ge(qklo_done, 2)
            load_head(3, 1)
            sp.dma_start(b1_sb[:], b1).then_inc(bias_in, 16)
            sp.dma_start(b2_sb[:], b2.rearrange("(a d) -> a d", a=1).broadcast_to([P, D])).then_inc(bias_in, 16)
            pair_steps(0, 2, True)
            with sp.Fori(1, PAIRS - 2) as pair:
                pair_steps(pair, 2)
            pair_steps(PAIRS - 2, 1)
            pair_steps(PAIRS - 1, 0)
            for c in range(NT // 2):
                sp.wait_ge(fin_done, c + 1)
                sp.dma_start(ov[:, 2 * c:2 * c + 2], final[:, 2 * c:2 * c + 2]).then_inc(out_done, 16)
            sp.wait_ge(out_done, 16 * (NT // 2))

        @block.tensor
        def _(pe):
            mm = nc.tensor.matmul

            def transpose_x(ln, half):
                banks = (SC, PR)[ln]
                for kd in range(KD):
                    if half == 1:
                        pe.wait_ge(xt_lo_done, ln * 4 + kd + 1)
                    if kd == 0:
                        pe.wait_ge(xn_ready, ln * NT + half * 4 + 4)
                    for t in range(4):
                        last = nc.tensor.transpose(banks[kd][:, t * P:(t + 1) * P],
                                                   xnorm[:, half * 4 + t, kd * P:(kd + 1) * P], ident_sb[:])
                    last.then_inc(xt_ready, 1)

            def project(head, a, c, m):
                if c == 0:
                    pe.wait_ge(qklo_done, head + 1)
                if not (isinstance(m, int) and m < 2):
                    pe.wait_ge(proj_copied, m - 1)
                n = 0
                for kd in range(KD):
                    for wt, xt in ((qk_lo[a], xT_hi), (qk_hi[a], xT_lo), (qk_hi[a], xT_hi)):
                        last = mm(PR[c % 2][:], wt[:, c % 2, kd], xt[:, kd, half_of(c)],
                                  start=(n == 0), stop=(n == 3 * KD - 1))
                        n += 1
                last.then_inc(proj_done, 1)

            def project_v(pair, c, v):
                if c == 0:
                    pe.wait_ge(vlo_done, pair + 1)
                if c >= 2:
                    pe.wait_ge(v_copied, v - 1)
                elif not (isinstance(v, int) and v < 8):
                    pe.wait_ge(wo_added, v - 5)
                for i in range(2):
                    t = 2 * c + i
                    n = 0
                    for kd in range(KD):
                        for xt, wt in ((xT_hi, v_lo), (xT_lo, v_hi), (xT_hi, v_hi)):
                            last = mm(VO[c % 2][:, i * 256:(i + 1) * 256], xt[:, kd, t * P:(t + 1) * P], wt[:, kd],
                                      start=(n == 0), stop=(n == 3 * KD - 1))
                            n += 1
                last.then_inc(v_done, 1)

            def scores(n, head, a, j):
                if j == 0:
                    pe.wait_ge(rotlo_done, 4 * head + 2)
                if j == 2:
                    pe.wait_ge(rotlo_done, 4 * head + 4)
                if not (isinstance(n, int) and n < 2):
                    pe.wait_ge(exp_done, 2 * n - 2)
                for i in range(2):
                    t = 2 * j + i
                    k0 = max(t - 1, 0)
                    o0 = i * 256 + (k0 - t + 1) * P
                    terms = ((rot_lo(a, 0), rot_hi(a, 1)), (rot_hi(a, 0), rot_lo(a, 1)), (rot_hi(a, 0), rot_hi(a, 1)))
                    for p_, (q, k) in enumerate(terms):
                        last = mm(SC[j % 2][:, o0:(i + 1) * 256], q[:, t * P:(t + 1) * P], k[:, k0 * P:(t + 1) * P],
                                  start=(p_ == 0), stop=(p_ == 2))
                last.then_inc(scores_done, 1)

            def transpose_probs(n, j):
                pe.wait_ge(scaled, n + 1)
                if not (isinstance(n, int) and n == 0):
                    pe.wait_ge(pt_masked, n)
                for i in range(2):
                    last = nc.tensor.transpose(PT[:, i * P:(i + 1) * P], probs[j % 2][:, i], ident_sb[:])
                last.then_inc(pt_done, 1)

            def weigh_v(n, pair, a, j):
                pe.wait_ge(pt_masked, n + 1)
                pe.wait_ge(v_copied, 4 * pair + j + 1)
                if not (isinstance(n, int) and n == 0):
                    pe.wait_ge(otlo_done, n)
                for i in range(2):
                    t = 2 * j + i
                    b0 = 1 if t == 0 else 0
                    for b in range(b0, 2):
                        last = mm(OT[:, i * P:(i + 1) * P], v_sb[:, t - 1 + b, a * HD:(a + 1) * HD],
                                  probsT[:, i, b], start=(b == b0), stop=(b == 1))
                last.then_inc(pv_done, 1)

            def project_out(pair, c, w, last_pair=False):
                if c == 0:
                    pe.wait_ge(olo_done, pair + 1)
                pe.wait_ge(otlo_done, 8 * pair + 5 + c)
                if c >= 2 or last_pair:
                    pe.wait_ge(wo_added, w - 1)
                    if last_pair and c == 1:
                        pe.wait_ge(mean_read, 2)
                else:
                    pe.wait_ge(v_copied, w + 7)
                for i in range(2):
                    t = 2 * c + i
                    n = 0
                    for a in range(2):
                        for ot, wt in ((oT_hi(a), o_lo), (oT_lo(a), o_hi), (oT_hi(a), o_hi)):
                            last = mm(VO[c % 2][:, i * 256:(i + 1) * 256], ot[:, t * P:(t + 1) * P], wt[:, a],
                                      start=(n == 0), stop=(n == 5))
                            n += 1
                last.then_inc(wo_done, 1)

            def means_of_abs():
                pe.wait_ge(abs_done, 8)
                pe.wait_ge(wo_added, 4 * PAIRS - 4)
                mm(VO[1][:, 0:8], mean_ones[:], abs_sum[:].rearrange("p k i -> p (k i)"),
                   start=True, stop=True).then_inc(mean_done, 1)

            def pair_steps(pair, first, last):
                for s in range(8):
                    n = 8 * pair + s
                    a, j = s // 4, s % 4
                    pa, pj = before(s)
                    if not (first and s == 0):
                        transpose_probs(n - 1, pj)
                    if not (last and s >= 4):
                        project(2 * pair + a + 1, 1 - a, j, n + 4)
                    if 1 <= s <= 4 and not first:
                        project_out(pair - 1, s - 1, 4 * pair - 5 + s)
                    if s == 0:
                        project_v(pair, 3, 4 * pair + 3)
                    if s >= 5 and not last:
                        project_v(pair + 1, s - 5, 4 * pair + s - 1)
                    early = s % 2 == 0 or (last and s == 5)
                    if early:
                        scores(n + 1, 2 * pair + (s + 1) // 4, (s + 1) // 4 % 2, (s + 1) % 4)
                    if not (first and s == 0):
                        weigh_v(n - 1, pair if s > 0 else pair - 1, pa, pj)
                    if not early and not (last and s == 7):
                        scores(n + 1, 2 * pair + (s + 1) // 4, (s + 1) // 4 % 2, (s + 1) % 4)
                    if s == 5 and last:
                        means_of_abs()
                    if s >= 6 and last:
                        project_out(pair, s - 6, 4 * pair + s - 6, True)

            pe.wait_ge(ident_in, 16)
            transpose_x(0, 0)
            pe.wait_ge(xt_lo_done, 2)
            project(0, 0, 0, 0)
            project(0, 0, 1, 1)
            transpose_x(0, 1)
            project_v(0, 0, 0)
            project_v(0, 1, 1)
            pe.wait_ge(xt_lo_done, 4)
            project(0, 0, 2, 2)
            project(0, 0, 3, 3)
            project_v(0, 2, 2)
            scores(0, 0, 0, 0)
            pair_steps(0, True, False)
            with pe.Fori(1, PAIRS - 1) as pair:
                pair_steps(pair, False, False)
            pair_steps(PAIRS - 1, False, True)
            transpose_probs(LAST, 3)
            project_out(PAIRS - 1, 2, 4 * PAIRS - 2, True)
            weigh_v(LAST, PAIRS - 1, 1, 3)
            transpose_x(1, 0)
            project_out(PAIRS - 1, 3, 4 * PAIRS - 1)

            hb = [SC[0], SC[1], VO[0], VO[1]]
            for half in range(2):
                pe.wait_ge(xt_lo_done, 4 + 2 * half + 2)
                for f in range(NF):
                    k = half * NF + f
                    if k % 4 == 0 and half == 0:
                        pe.wait_ge(tern_done[0], k // 4 + 1)
                    if k in (2, 3):
                        pe.wait_ge(wo_added, 4 * PAIRS - 3 + k)
                    if k >= 4:
                        pe.wait_ge(gelu_done, k - 3)
                    for kd in range(KD):
                        for p_, xt in enumerate((xT_lo, xT_hi)):
                            last = mm(hb[k % 4][:], w1_sb[:, kd, f * P:(f + 1) * P],
                                      xt[:, kd, half * HALF:(half + 1) * HALF],
                                      start=(kd == 0 and p_ == 0), stop=(kd == KD - 1 and p_ == 1))
                    last.then_inc(h_done, 1)
                    if k == 4:
                        transpose_x(1, 1)
            yb = [OT, PT, PR[0], PR[1]]
            pe.wait_ge(tern_done[1], 1)
            for c in range(NT // 2):
                pe.wait_ge(glo_done[0], (c // 2 + 1) * (NF - NF // 4))
                pe.wait_ge(glo_done[1], (c // 2 + 1) * (NF // 4))
                for i in range(2):
                    t = 2 * c + i
                    for f in range(NF):
                        for p_, gt in enumerate((gT_lo, gT_hi)):
                            last = mm(yb[c][:, i * 256:(i + 1) * 256], gt[:, f, t * P:(t + 1) * P], w2_sb[:, f],
                                      start=(f == 0 and p_ == 0), stop=(f == NF - 1 and p_ == 1))
                last.then_inc(y_done, 1)

        @block.scalar
        def _(act):
            copy = nc.scalar.copy

            def xt_hi(ln, half):
                banks = (SC, PR)[ln]
                for kd in range(KD):
                    act.wait_ge(xt_ready, ln * 4 + half * 2 + kd + 1)
                    copy(xT_hi[:, kd, half * HALF:(half + 1) * HALF], banks[kd][:]).then_inc(xt_hi_done, 1)

            def qkhi(a, loads, head, reused):
                act.wait_ge(qk_in[a], 32 * loads)
                if reused:
                    act.wait_ge(proj_done, 4 * (head - 1))
                copy(qk_hi[a][:], qk_raw[a][:]).then_inc(qkhi_done, 1)

            def vhi(pair, reused):
                act.wait_ge(v_in, 16 * (pair + 1))
                if reused:
                    act.wait_ge(v_done, 4 * pair)
                copy(v_hi[:], v_raw[:]).then_inc(vhi_done, 1)

            def ohi(pair, reused):
                act.wait_ge(o_in, 16 * (pair + 1))
                if reused:
                    act.wait_ge(wo_done, 4 * pair)
                copy(o_hi[:], o_raw[:]).then_inc(ohi_done, 1)

            def copy_proj(c, m):
                act.wait_ge(proj_done, m + 1)
                if not (isinstance(m, int) and m < 4):
                    act.wait_ge(rotlo_done, m - 3)
                copy(turn[c][:], PR[c % 2][:]).then_inc(proj_copied, 1)

            def rothi(a, c, m):
                act.wait_ge(rot_done, m + 1)
                copy(rot_hi(a, c % 2)[:, half_of(c)], turn[c][:]).then_inc(rothi_done, 1)

            def exps(n, j):
                act.wait_ge(negmax_done, n + 1)
                for i in range(2):
                    nc.scalar.activation(probs[j % 2][:, i], SC[j % 2][:, i * 256 + P:(i + 1) * 256], ACT.Exp,
                                         bias=negmax[:, j % 2, i:i + 1], scale=SCALE,
                                         accum_out=rowsum[:, j % 2, i:i + 1]).then_inc(exp_done, 1)

            def scale_probs(n, j):
                act.wait_ge(rinv_done, n + 1)
                for i in range(2):
                    last = nc.scalar.activation(probs[j % 2][:, i], probs[j % 2][:, i], ACT.Copy,
                                                scale=rinv[:, j % 2, i:i + 1])
                last.then_inc(scaled, 1)

            def copy_v(c, v):
                act.wait_ge(v_done, v + 1)
                copy(v_sb[:, 2 * c:2 * c + 2], VO[c % 2][:].rearrange("p (t n) -> p t n", t=2)).then_inc(v_copied, 1)

            def ot_hi(n, a, j):
                act.wait_ge(pv_done, n + 1)
                copy(oT_hi(a)[:, 2 * j * P:(2 * j + 2) * P], OT[:, 0:256]).then_inc(othi_done, 1)

            def abs_sums(k, i):
                act.wait_ge(w12_in[k], 16 * (k + 1))
                raw = (w1_raw, w2_raw)[k]
                dest = (w1_sb, w2_sb)[k][:].rearrange("p a b -> p (a b)")
                cs = slice(i * NW // P // 4, (i + 1) * NW // P // 4)
                nc.scalar.activation(dest[:, cs], raw[:, cs], ACT.Abs,
                                     accum_out=abs_sum[:, k, i:i + 1]).then_inc(abs_done, 1)

            def pair_steps(pair, first, last):
                for s in range(8):
                    n = 8 * pair + s
                    m = n + 4
                    a, j = s // 4, s % 4
                    if not (last and s >= 6):
                        a2, c2 = before(s + 4, 2)
                        rothi(a2, c2, m - 2)
                    exps(n, j)
                    if not (last and s >= 4):
                        copy_proj(j, m)
                    scale_probs(n, j)
                    if not (first and s == 0):
                        ot_hi(n - 1, *before(s))
                    if s == 0 and not first:
                        copy_v(2, 4 * pair + 2)
                    if s == 1:
                        copy_v(3, 4 * pair + 3)
                    if s >= 6 and not last:
                        copy_v(s - 6, 4 * pair + s - 2)
                    if s == 1 and not last:
                        qkhi(0, pair + 2, 2 * pair + 2, True)
                    if s == 5 and not last:
                        qkhi(1, pair + 2, 2 * pair + 3, True)
                    if s == 3 and not last:
                        vhi(pair + 1, True)
                    if s == (4 if last else 6):
                        ohi(pair, not first)
                    if first:
                        abs_sums(s // 4, s % 4)

            nc.scalar.preload_act_table(ACT.Exp)
            qkhi(0, 1, 0, False)
            vhi(0, False)
            xt_hi(0, 0)
            qkhi(1, 1, 1, False)
            copy_proj(0, 0)
            copy_proj(1, 1)
            xt_hi(0, 1)
            copy_v(0, 0)
            copy_v(1, 1)
            rothi(0, 0, 0)
            copy_proj(2, 2)
            rothi(0, 1, 1)
            copy_proj(3, 3)
            copy_v(2, 2)
            pair_steps(0, True, False)
            with act.Fori(1, PAIRS - 1) as pair:
                pair_steps(pair, False, False)
            pair_steps(PAIRS - 1, False, True)
            nc.scalar.preload_act_table(ACT.Gelu)
            ot_hi(LAST, 1, 3)
            xt_hi(1, 0)
            act.wait_ge(bias_in, 32)
            hb = [SC[0], SC[1], VO[0], VO[1]]
            for k in range(2 * NF):
                f = k % NF
                act.wait_ge(h_done, k + 1)
                if k >= 4:
                    act.wait_ge(glo_done[1 if k % 4 == 3 else 0], glo_count(k - 4))
                nc.scalar.activation(gelu_tmp[k % 4][:], hb[k % 4][:], ACT.Gelu,
                                     bias=b1_sb[:, f:f + 1]).then_inc(gelu_done, 1)
                if k == 4:
                    xt_hi(1, 1)

        @block.vector
        def _(dve):
            tt = nc.vector.tensor_tensor

            def norm_stats(ln, half):
                hs = slice(half * 4, half * 4 + 4)
                for t in range(half * 4, half * 4 + 4):
                    if ln == 0 and t % 2 == 0:
                        dve.wait_ge(x_in[t // 2], 16)
                    if ln == 1 and t % 2 == 0:
                        dve.wait_ge(wo_added, 4 * PAIRS - 3 + t // 2)
                    nc.vector.bn_stats(stats[:, t], xres[:, t]).then_inc(bn_done, 1)
                for t in range(half * 4, half * 4 + 4):
                    dve.wait_ge(bn_done, ln * NT + t + 1)
                    nc.vector.bn_aggr(mv[:, t], stats[:, t]).then_inc(aggr_done, 1)
                dve.wait_ge(aggr_done, ln * NT + half * 4 + 4)
                nc.vector.tensor_scalar(var_eps[:, hs], mv[:, hs, 1], EPS_LN, None, ALU.add).then_inc(var_ready, 1)

            def normalise(ln, half):
                dve.wait_ge(rstd_ready, 2 * ln + half + 1)
                for t in range(half * 4, half * 4 + 4):
                    nc.vector.tensor_scalar(xnorm[:, t], xres[:, t], mv[:, t, 0:1], rstd[:, t:t + 1],
                                            ALU.subtract, ALU.mult).then_inc(xn_ready, 1)

            def xt_lo(ln, half):
                banks = (SC, PR)[ln]
                hs = slice(half * HALF, (half + 1) * HALF)
                for kd in range(KD):
                    dve.wait_ge(xt_hi_done, ln * 4 + half * 2 + kd + 1)
                    tt(xT_lo[:, kd, hs], banks[kd][:], xT_hi[:, kd, hs].bitcast(F32),
                       ALU.subtract).then_inc(xt_lo_done, 1)

            def times_cos(c, m, swaps):
                dve.wait_ge(swap_in[c], 32 * swaps)
                tt(turn[c][:], turn[c][:], cos_sb[:, half_of(c)], ALU.mult).then_inc(cos_done, 1)

            def rotate(c):
                if c == 0:
                    dve.wait_ge(tab_in[0], 32)
                times_cos(c, c, 1)
                tt(swapped[c][:], swapped[c][:], sin_sb[:, half_of(c)], ALU.mult).then_inc(sin_done, 1)
                dve.wait_ge(sin_done, c + 1)
                tt(turn[c][:], turn[c][:], swapped[c][:], ALU.add).then_inc(rot_done, 1)

            def rotlo(a, c, m):
                dve.wait_ge(rothi_done, m + 1)
                tt(rot_lo(a, c % 2)[:, half_of(c)], turn[c][:], rot_hi(a, c % 2)[:, half_of(c)].bitcast(F32),
                   ALU.subtract).then_inc(rotlo_done, 1)

            def merge(n, j, first_in_loop):
                if first_in_loop:
                    dve.wait_ge(scores_done, n + 1)
                    nc.vector.memset(rowsum[:, j % 2], 0.0)
                else:
                    dve.wait_ge(mask_in, 32)
                    dve.wait_ge(scores_done, n + 1)
                sc = SC[j % 2][:].rearrange("p (i b k) -> p i b k", i=2, b=2)
                if j == 0:
                    nc.vector.copy_predicated(sc[:, 0, 1], in_prev_sb[:], nothing[:])
                    nc.vector.copy_predicated(sc[:, 1, 1], in_prev_sb[:], sc[:, 1, 0]).then_inc(merged, 1)
                else:
                    nc.vector.copy_predicated(sc[:, :, 1], in_prev_sb[:].unsqueeze(1).broadcast_to([P, 2, P]),
                                              sc[:, :, 0]).then_inc(merged, 1)
                dve.wait_ge(merged, n + 1)
                nc.vector.tensor_reduce(rowmax[:, j % 2], sc[:, :, 1], AX.X, ALU.max).then_inc(max_done, 1)
                dve.wait_ge(max_done, n + 1)
                nc.vector.tensor_scalar(negmax[:, j % 2], rowmax[:, j % 2], -SCALE, None,
                                        ALU.mult).then_inc(negmax_done, 1)

            def inverse_sum(n, j):
                dve.wait_ge(exp_done, 2 * n + 2)
                nc.vector.reciprocal(rinv[:, j % 2], rowsum[:, j % 2]).then_inc(rinv_done, 1)

            def mask_pt(n):
                dve.wait_ge(pt_done, n + 1)
                if not (isinstance(n, int) and n == 0):
                    dve.wait_ge(pv_done, n)
                tt(probsT[:], PT[:, 0:256].rearrange("p (i q) -> p i q", i=2).unsqueeze(2).broadcast_to([P, 2, 2, P]),
                   mask_sb[:].unsqueeze(1).broadcast_to([P, 2, 2, P]), ALU.mult).then_inc(pt_masked, 1)

            def ot_lo(n, a, j):
                dve.wait_ge(othi_done, n + 1)
                ts = slice(2 * j * P, (2 * j + 2) * P)
                tt(oT_lo(a)[:, ts], OT[:, 0:256], oT_hi(a)[:, ts].bitcast(F32), ALU.subtract).then_inc(otlo_done, 1)

            def add_out(c, w):
                dve.wait_ge(wo_done, w + 1)
                ts = slice(2 * c, 2 * c + 2)
                tt(xres[:, ts], VO[c % 2][:].rearrange("p (t d) -> p t d", t=2), xres[:, ts], ALU.add).then_inc(wo_added, 1)

            def thresholds():
                dve.wait_ge(mean_done, 1)
                for k in range(2):
                    nc.vector.tensor_reduce(mean_abs[:, k:k + 1], VO[1][:, 4 * k:4 * k + 4], AX.X,
                                            ALU.add).then_inc(mean_read, 1)
                dve.wait_ge(mean_read, 2)
                nc.vector.tensor_scalar(thr[:, :, 0], mean_abs[:], EPS_Q, 0.5, ALU.max, ALU.mult)
                nc.vector.tensor_scalar(thr[:, :, 1], mean_abs[:], EPS_Q, -0.5, ALU.max, ALU.mult).then_inc(thr_done, 1)

            def ternary_w1(part):
                if part == 0:
                    dve.wait_ge(thr_done, 1)
                fs = slice(part * F // 2, (part + 1) * F // 2)
                raw = w1_raw[:].rearrange("p (k f) -> p k f", k=KD)[:, :, fs]
                dest = w1_sb[:, :, fs]
                nc.vector.tensor_scalar(dest, raw, thr[:, 0, 1:2], None, ALU.is_lt).then_inc(below_done[0], 1)
                dve.wait_ge(below_done[0], part + 1)
                nc.vector.scalar_tensor_tensor(dest, raw, thr[:, 0, 0:1], dest.bitcast(F32), ALU.is_gt,
                                               ALU.subtract).then_inc(tern_done[0], 1)

            def pair_steps(pair, first, last):
                for s in range(8):
                    n = 8 * pair + s
                    m = n + 4
                    j = s % 4
                    merge(n, j, s < 2 and not isinstance(n, int))
                    if not (first and s == 0):
                        mask_pt(n - 1)
                    if not (last and s >= 6):
                        rotlo(*before(s + 4, 2), m - 2)
                    inverse_sum(n, j)
                    if not (last and s >= 5):
                        c1 = (s - 1) % 4
                        times_cos(c1, m - 1, 2 * pair + (s + 3) // 4 + 1)
                    if 1 <= s <= 4 and not first:
                        add_out(s - 1, 4 * pair - 5 + s)
                    if not (first and s == 0):
                        ot_lo(n - 1, *before(s))
                    if s == 5 and last:
                        thresholds()
                    if s == 6 and last:
                        ternary_w1(0)
                    if s >= 6 and last:
                        add_out(s - 6, 4 * pair + s - 6)

            nc.vector.memset(mean_ones[:], 1.0 / NW)
            nc.vector.memset(minus_half[:], -0.5).then_inc(consts_set, 1)
            norm_stats(0, 0)
            normalise(0, 0)
            norm_stats(0, 1)
            xt_lo(0, 0)
            normalise(0, 1)
            rotate(0)
            xt_lo(0, 1)
            rotate(1)
            rotlo(0, 0, 0)
            rotlo(0, 1, 1)
            dve.wait_ge(tab_in[1], 32)
            times_cos(2, 2, 1)
            dve.wait_ge(nothing_set, 1)
            dve.wait_ge(mask_in, 32)
            pair_steps(0, True, False)
            with dve.Fori(1, PAIRS - 1) as pair:
                pair_steps(pair, False, False)
            pair_steps(PAIRS - 1, False, True)
            norm_stats(1, 0)
            mask_pt(LAST)
            add_out(2, 4 * PAIRS - 2)
            normalise(1, 0)
            ot_lo(LAST, 1, 3)
            ternary_w1(1)
            xt_lo(1, 0)
            add_out(3, 4 * PAIRS - 1)
            norm_stats(1, 1)

            def ghi(k):
                hs = slice((k // NF) * HALF, (k // NF + 1) * HALF)
                dve.wait_ge(gelu_done, k + 1)
                nc.vector.tensor_copy(gT_hi[:, k % NF, hs], gelu_tmp[k % 4][:]).then_inc(ghi_done, 1)

            def glo(k):
                hs = slice((k // NF) * HALF, (k // NF + 1) * HALF)
                dve.wait_ge(ghi_done, k + 1)
                tt(gT_lo[:, k % NF, hs], gelu_tmp[k % 4][:], gT_hi[:, k % NF, hs].bitcast(F32),
                   ALU.subtract).then_inc(glo_done[0], 1)

            ghi(0)
            normalise(1, 1)
            for k in range(2 * NF):
                if k + 1 < 2 * NF:
                    ghi(k + 1)
                if k % 4 != 3:
                    glo(k)
                if k == 3:
                    xt_lo(1, 1)
            yb = [OT, PT, PR[0], PR[1]]
            dve.wait_ge(b2_added, NT)
            for c in range(NT // 2):
                dve.wait_ge(y_done, c + 1)
                tt(final[:, 2 * c:2 * c + 2], yb[c][:].rearrange("p (t d) -> p t d", t=2), xres[:, 2 * c:2 * c + 2],
                   ALU.add).then_inc(fin_done, 1)

        @block.gpsimd
        def _(pool):
            tt = nc.gpsimd.tensor_tensor

            def rsqrt(ln, half):
                hs = slice(half * 4, half * 4 + 4)
                pool.wait_ge(var_ready, 2 * ln + half + 1)
                tt(rstd[:, hs], var_eps[:, hs], minus_half[:, hs], ALU.pow).then_inc(rstd_ready, 1)

            def qklo(a, head):
                pool.wait_ge(qkhi_done, head + 1)
                tt(qk_lo[a][:], qk_raw[a][:], qk_hi[a][:].bitcast(F32), ALU.subtract).then_inc(qklo_done, 1)

            def vlo(pair):
                pool.wait_ge(vhi_done, pair + 1)
                tt(v_lo[:], v_raw[:], v_hi[:].bitcast(F32), ALU.subtract).then_inc(vlo_done, 1)

            def olo(pair):
                pool.wait_ge(ohi_done, pair + 1)
                tt(o_lo[:], o_raw[:], o_hi[:].bitcast(F32), ALU.subtract).then_inc(olo_done, 1)

            def rotate(c, m, swaps):
                pool.wait_ge(swap_in[c], 32 * swaps)
                tt(swapped[c][:], swapped[c][:], sin_sb[:, half_of(c)], ALU.mult).then_inc(sin_done, 1)
                pool.wait_ge(cos_done, m + 1)
                pool.wait_ge(sin_done, m + 1)
                tt(turn[c][:], turn[c][:], swapped[c][:], ALU.add).then_inc(rot_done, 1)

            def ternary_w2():
                dest = w2_sb[:].rearrange("p a b -> p (a b)")
                pool.wait_ge(thr_done, 1)
                nc.gpsimd.tensor_scalar(dest, w2_raw[:], thr[:, 1, 1:2], None, ALU.is_lt).then_inc(below_done[1], 1)
                nc.gpsimd.tensor_scalar(w2_raw[:], w2_raw[:], thr[:, 1, 0:1], None, ALU.is_gt).then_inc(above_done, 1)
                rsqrt(1, 0)
                pool.wait_ge(below_done[1], 1)
                pool.wait_ge(above_done, 1)
                tt(dest, w2_raw[:], dest.bitcast(F32), ALU.subtract).then_inc(tern_done[1], 1)

            def pair_steps(pair, first, last):
                for s in range(8):
                    m = 8 * pair + s + 4
                    if not (last and s >= 5):
                        rotate((s - 1) % 4, m - 1, 2 * pair + (s + 3) // 4 + 1)
                    if s == 1 and not last:
                        qklo(0, 2 * pair + 2)
                    if s == 5 and not last:
                        qklo(1, 2 * pair + 3)
                    if s == 3 and not last:
                        vlo(pair + 1)
                    if s == (4 if last else 6):
                        olo(pair)

            nc.gpsimd.memset(nothing[:], -BIG).then_inc(nothing_set, 1)
            pool.wait_ge(consts_set, 1)
            rsqrt(0, 0)
            qklo(0, 0)
            rsqrt(0, 1)
            vlo(0)
            qklo(1, 1)
            pool.wait_ge(tab_in[1], 32)
            pool.wait_ge(rot_done, 2)
            rotate(2, 2, 1)
            pair_steps(0, True, False)
            with pool.Fori(1, PAIRS - 1) as pair:
                pair_steps(pair, False, False)
            pair_steps(PAIRS - 1, False, True)
            ternary_w2()
            rsqrt(1, 1)
            pool.wait_ge(bias_in, 32)
            for k in range(2 * NF):
                hs = slice((k // NF) * HALF, (k // NF + 1) * HALF)
                if k % 4 == 3:
                    pool.wait_ge(ghi_done, k + 1)
                    tt(gT_lo[:, k % NF, hs], gelu_tmp[k % 4][:], gT_hi[:, k % NF, hs].bitcast(F32),
                       ALU.subtract).then_inc(glo_done[1], 1)
                if k < NT:
                    pool.wait_ge(xn_ready, NT + k + 1)
                    tt(xres[:, k], xres[:, k], b2_sb[:], ALU.add).then_inc(b2_added, 1)


def tables(T, HD):
    import numpy as np
    inv_freq = (np.float32(1.0) / np.power(np.float32(10000.0), np.arange(0, HD, 2, dtype=np.float32) / np.float32(HD))).astype(np.float32)
    freqs = np.arange(T, dtype=np.float32)[:, None] * inv_freq[None, :]
    c, s = np.cos(freqs).astype(np.float32).T, np.sin(freqs).astype(np.float32).T
    q = np.arange(HD)[:, None]
    k = np.arange(HD)[None, :]
    prev = k > q
    mask_t = np.concatenate([prev.T, ~prev.T], 1)
    return {"cos_t": np.concatenate([c, c], 0), "sin_t": np.concatenate([-s, s], 0),
            "in_prev": prev.astype(np.int32), "mask_t": mask_t.astype(np.float32), "ident": np.eye(HD, dtype=np.float32)}


def kernel(L0_attn_hidden_states, L0_attn_wq, L0_attn_wk, L0_attn_wv, L0_attn_wo, L0_ffn_w1, L0_ffn_b1, L0_ffn_w2,
           L0_ffn_b2):
    import numpy as np
    import concourse.bacc as bacc
    from concourse.bass_utils import run_bass_kernel_spmd as run

    x = np.asarray(L0_attn_hidden_states)
    arrays = {"x": x[0], "wq": L0_attn_wq, "wk": L0_attn_wk, "wv": L0_attn_wv, "wo": L0_attn_wo,
              "w1t": np.asarray(L0_ffn_w1).T, "b1": np.asarray(L0_ffn_b1).reshape(-1, P).T, "w2t": np.asarray(L0_ffn_w2).T, "b2": L0_ffn_b2,
              **tables(x.shape[1], P)}
    arrays = {k: np.ascontiguousarray(v) for k, v in arrays.items()}
    nc = bacc.Bacc("TRN2", target_bir_lowering=False, num_devices=1)
    args = {k: nc.dram_tensor(f"in_{k}", v.shape, mybir.dt.from_np(v.dtype), kind="ExternalInput").ap()
            for k, v in arrays.items()}
    out = nc.dram_tensor("out_y", x[0].shape, F32, kind="ExternalOutput").ap()
    preln_block_kernel(nc, out=out, **args)
    r = run(nc, [{f"in_{k}": v for k, v in arrays.items()}], core_ids=[0])
    return r.results[0]["out_y"].reshape(x.shape)
```

```python
from contextlib import ExitStack

import concourse.bass as bass
from concourse import mybir

P = 128
ALU = mybir.AluOpType
ACT = mybir.ActivationFunctionType
AX = mybir.AxisListType
F32 = mybir.dt.float32
F32R = mybir.dt.float32r
BIG = 3.4028234663852886e38


def preln_block_kernel(nc, x, wq, wk, wv, wo, w1t, b1, w2t, b2, cos_t, sin_t, in_prev, mask_t, ident, out):
    T, D = x.shape
    HD = P
    HEADS = wq.shape[1] // HD
    PAIRS = HEADS // 2
    NT = T // P
    KD = D // P
    F = w1t.shape[1]
    NF = F // P
    HALF = T // 2
    SCALE = float(HD) ** -0.5
    EPS_LN = 1e-5
    EPS_Q = 1e-8
    NW = D * F
    CHUNKS = 4 * HEADS
    LAST = 8 * PAIRS - 1
    assert T == 1024 and D == 256 and F == 1024

    with ExitStack() as ctx:
        def sb(name, shape, dt=F32):
            return ctx.enter_context(nc.sbuf_tensor(name, shape, dt))

        def bank(name):
            return ctx.enter_context(nc.psum_tensor(name, [P, 512], F32))

        def sem(name):
            return ctx.enter_context(nc.semaphore(name))

        xres = sb("xres", [P, NT, D])
        xnorm = sb("xnorm", [P, NT, D])
        xT_hi = sb("xT_hi", [P, KD, T], F32R)
        xT_lo = sb("xT_lo", [P, KD, T], F32R)
        qk_raw = [sb(f"qk_raw{a}", [P, 2, KD, HD]) for a in range(2)]
        qk_hi = [sb(f"qk_hi{a}", [P, 2, KD, HD], F32R) for a in range(2)]
        qk_lo = [sb(f"qk_lo{a}", [P, 2, KD, HD], F32R) for a in range(2)]
        v_raw = sb("v_raw", [P, KD, 2 * HD])
        v_hi = sb("v_hi", [P, KD, 2 * HD], F32R)
        v_lo = sb("v_lo", [P, KD, 2 * HD], F32R)
        o_raw = sb("o_raw", [P, 2, D])
        o_hi = sb("o_hi", [P, 2, D], F32R)
        o_lo = sb("o_lo", [P, 2, D], F32R)
        turn = [sb(f"turn{c}", [P, 512]) for c in range(4)]
        swapped = [sb(f"swapped{c}", [P, 512]) for c in range(4)]
        cos_sb = sb("cos_sb", [P, T])
        sin_sb = sb("sin_sb", [P, T])
        in_prev_sb = sb("in_prev_sb", [P, P], mybir.dt.int32)
        mask_sb = sb("mask_sb", [P, 2, P])
        nothing = sb("nothing", [P, P])
        ident_sb = sb("ident_sb", [P, P])
        probs = [sb(f"probs{i}", [P, 2, P]) for i in range(2)]
        rowmax = sb("rowmax", [P, 2, 2])
        negmax = sb("negmax", [P, 2, 2])
        rowsum = sb("rowsum", [P, 2, 2])
        rinv = sb("rinv", [P, 2, 2])
        probsT = sb("probsT", [P, 2, 2, P])
        v_sb = sb("v_sb", [P, NT, 2 * HD])
        gT_hi = sb("gT_hi", [P, NF, T], F32R)
        gT_lo = sb("gT_lo", [P, NF, T], F32R)

        def rot_hi(a, w):
            return gT_hi[:, 2 * a + w]

        def rot_lo(a, w):
            return gT_lo[:, 2 * a + w]

        def oT_hi(a):
            return gT_hi[:, 4 + a]

        def oT_lo(a):
            return gT_lo[:, 4 + a]

        w1_raw = sb("w1_raw", [P, KD * F])
        w2_raw = sb("w2_raw", [P, NF * D])
        cos_product = w2_raw
        w1_sb = sb("w1_sb", [P, KD, F], F32R)
        w2_sb = sb("w2_sb", [P, NF, D], F32R)
        b1_sb = sb("b1_sb", [P, NF])
        b2_sb = sb("b2_sb", [P, D])
        stats = sb("stats", [P, NT, 6])
        mv = sb("mv", [P, NT, 2])
        rstd = sb("rstd", [P, NT])
        var_eps = sb("var_eps", [P, NT])
        minus_half = sb("minus_half", [P, NT])
        mean_ones = sb("mean_ones", [P, P])
        abs_sum = sb("abs_sum", [P, 2, 4])
        mean_abs = sb("mean_abs", [P, 2])
        thr = sb("thr", [P, 2, 2])
        gelu_tmp = turn
        final = xnorm

        PR = [bank(f"PR{i}") for i in range(2)]
        SC = [bank(f"SC{i}") for i in range(2)]
        PT = bank("PT")
        OT = bank("OT")
        VO = [bank(f"VO{i}") for i in range(2)]

        x_in = [sem(f"x_in{i}") for i in range(4)]
        tab_in = [sem(f"tab_in{i}") for i in range(2)]
        mask_in = sem("mask_in")
        ident_in = sem("ident_in")
        bias_in = sem("bias_in")
        w12_in = [sem(f"w{k + 1}_in") for k in range(2)]
        qk_in = [sem(f"qk_in{a}") for a in range(2)]
        v_in = sem("v_in")
        o_in = sem("o_in")
        swap_in = [sem(f"swap_in{c}") for c in range(4)]
        consts_set = sem("consts_set")
        nothing_set = sem("nothing_set")
        bn_done = sem("bn_done")
        aggr_done = sem("aggr_done")
        var_ready = sem("var_ready")
        rstd_ready = sem("rstd_ready")
        xn_ready = sem("xn_ready")
        xt_ready = sem("xt_ready")
        xt_hi_done = sem("xt_hi_done")
        xt_lo_done = sem("xt_lo_done")
        qkhi_done = sem("qkhi_done")
        qklo_done = sem("qklo_done")
        vhi_done = sem("vhi_done")
        vlo_done = sem("vlo_done")
        ohi_done = sem("ohi_done")
        olo_done = sem("olo_done")
        proj_done = sem("proj_done")
        proj_copied = sem("proj_copied")
        cos_done = sem("cos_done")
        sin_done = sem("sin_done")
        rot_done = sem("rot_done")
        rothi_done = sem("rothi_done")
        rotlo_done = sem("rotlo_done")
        scores_done = sem("scores_done")
        merged = sem("merged")
        max_done = sem("max_done")
        negmax_done = sem("negmax_done")
        exp_done = sem("exp_done")
        rinv_done = sem("rinv_done")
        scaled = sem("scaled")
        pt_done = sem("pt_done")
        pt_masked = sem("pt_masked")
        pv_done = sem("pv_done")
        othi_done = sem("othi_done")
        otlo_done = sem("otlo_done")
        v_done = sem("v_done")
        v_copied = sem("v_copied")
        wo_done = sem("wo_done")
        wo_added = sem("wo_added")
        abs_done = sem("abs_done")
        mean_done = sem("mean_done")
        mean_read = sem("mean_read")
        thr_done = sem("thr_done")
        below_done = [sem("w1_below_a"), sem("w2_below"), sem("w1_below_b")]
        above_done = sem("w1_above_a")
        tern_done = [sem("w1_ternary_a"), sem("w2_ternary"), sem("w1_ternary_b")]
        h_done = sem("h_done")
        gelu_done = sem("gelu_done")
        ghi_done = [sem("ghi_dve"), sem("ghi_act")]
        glo_done = [sem("glo_dve"), sem("glo_pool")]
        b2_added = sem("b2_added")
        y_done = sem("y_done")
        fin_done = sem("fin_done")
        out_done = sem("out_done")

        def half_of(c):
            return slice((c // 2) * HALF, (c // 2 + 1) * HALF)

        def before(s, d=1):
            return ((s - d) % 8) // 4, (s - d) % 4

        def hi_by(k):
            return (1, k // 4 + 1) if k % 4 == 3 else (0, k - k // 4 + 1)

        def lo_by(k):
            return k % 2, k // 2 + 1


        block = ctx.enter_context(nc.Block())

        @block.sync
        def _(sp):
            xv = x.rearrange("(t p) d -> p t d", p=P)
            ov = out.rearrange("(t p) d -> p t d", p=P)

            def load_head(head, a):
                for w, src in ((0, wq), (1, wk)):
                    s = src.rearrange("(k p) n -> p k n", p=P)
                    sp.dma_start(qk_raw[a][:, w], s[:, :, bass.ds(head * HD, HD)]).then_inc(qk_in[a], 16)

            def load_v(pair):
                s = wv.rearrange("(k p) n -> p k n", p=P)
                sp.dma_start(v_raw[:], s[:, :, bass.ds(pair * 2 * HD, 2 * HD)]).then_inc(v_in, 16)

            def load_o(pair):
                s = wo[bass.ds(pair * 2 * HD, 2 * HD), :].rearrange("(a p) n -> p a n", p=P)
                sp.dma_start(o_raw[:], s).then_inc(o_in, 16)

            def load_tables(half):
                hs = slice(half * HALF, (half + 1) * HALF)
                sp.dma_start(cos_sb[:, hs], cos_t[:, hs]).then_inc(tab_in[half], 16)
                sp.dma_start(sin_sb[:, hs], sin_t[:, hs]).then_inc(tab_in[half], 16)

            def swap(m, c):
                sp.wait_ge(proj_copied, m + 1)
                for to, fr in ((0, HD // 2), (HD // 2, 0)):
                    sp.dma_start(swapped[c][to:to + HD // 2, :],
                                 turn[c][fr:fr + HD // 2, :]).then_inc(swap_in[c], 16)

            def pair_steps(pair, ahead, first=False):
                for s in range(8):
                    if not (ahead == 0 and s >= 4):
                        swap(8 * pair + s + 4, s % 4)
                    if first and s in (1, 2):
                        sp.wait_ge(rot_done, 2)
                        h = NF // 2
                        fs = slice((s - 1) * h, s * h)
                        sp.dma_start(w2_raw[:].rearrange("p (f n) -> p f n", f=NF)[:, fs],
                                     w2t.rearrange("(f p) n -> p f n", p=P)[:, fs]).then_inc(w12_in[1], 16)
                    if s == 2 and ahead == 2:
                        sp.wait_ge(qklo_done, 2 * pair + 3)
                        load_head(2 * pair + 4, 0)
                    if s == 6 and ahead == 2:
                        sp.wait_ge(qklo_done, 2 * pair + 4)
                        load_head(2 * pair + 5, 1)
                    if s == 4 and ahead == 2:
                        sp.wait_ge(vlo_done, pair + 2)
                        load_v(pair + 2)
                    if s == 7 and ahead >= 1:
                        sp.wait_ge(olo_done, pair + 1)
                        load_o(pair + 1)

            for i in range(4):
                sp.dma_start(xres[:, 2 * i:2 * i + 2], xv[:, 2 * i:2 * i + 2]).then_inc(x_in[i], 16)
                if i == 0:
                    sp.dma_start(ident_sb[:], ident).then_inc(ident_in, 16)
                if i == 1:
                    load_head(0, 0)
            load_v(0)
            load_tables(0)
            load_head(1, 1)
            sp.dma_start(in_prev_sb[:], in_prev).then_inc(mask_in, 16)
            sp.dma_start(mask_sb[:].rearrange("p b q -> p (b q)"), mask_t).then_inc(mask_in, 16)
            load_tables(1)
            sp.wait_ge(qklo_done, 1)
            load_head(2, 0)
            swap(0, 0)
            swap(1, 1)
            sp.dma_start(w1_raw[:].rearrange("p (k f) -> p k f", k=KD),
                         w1t.rearrange("(k p) f -> p k f", p=P)).then_inc(w12_in[0], 16)
            sp.wait_ge(vlo_done, 1)
            load_v(1)
            load_o(0)
            swap(2, 2)
            swap(3, 3)
            sp.wait_ge(qklo_done, 2)
            load_head(3, 1)
            sp.dma_start(b1_sb[:], b1).then_inc(bias_in, 16)
            sp.dma_start(b2_sb[:], b2.rearrange("(a d) -> a d", a=1).broadcast_to([P, D])).then_inc(bias_in, 16)
            pair_steps(0, 2, True)
            with sp.Fori(1, PAIRS - 2) as pair:
                pair_steps(pair, 2)
            pair_steps(PAIRS - 2, 1)
            pair_steps(PAIRS - 1, 0)
            for c in range(NT // 2):
                sp.wait_ge(fin_done, c + 1)
                sp.dma_start(ov[:, 2 * c:2 * c + 2], final[:, 2 * c:2 * c + 2]).then_inc(out_done, 16)
            sp.wait_ge(out_done, 16 * (NT // 2))

        @block.tensor
        def _(pe):
            mm = nc.tensor.matmul

            def transpose_x(ln, half):
                banks = (SC, PR)[ln]
                if half == 1:
                    pe.wait_ge(xt_lo_done, ln * 4 + 2)
                for t in range(4):
                    pe.wait_ge(xn_ready, ln * NT + half * 4 + t + 1)
                    for kd in range(KD):
                        tr = nc.tensor.transpose(banks[kd][:, t * P:(t + 1) * P],
                                                 xnorm[:, half * 4 + t, kd * P:(kd + 1) * P], ident_sb[:])
                        if t == 3:
                            tr.then_inc(xt_ready, 1)

            def warm_up(products):
                for _ in range(products):
                    mm(VO[0][:, 0:P], mean_ones[:], mean_ones[:], start=True, stop=True)

            def project(head, a, c, m):
                if c == 0:
                    pe.wait_ge(qklo_done, head + 1)
                if not (isinstance(m, int) and m < 2):
                    pe.wait_ge(proj_copied, m - 1)
                n = 0
                for kd in range(KD):
                    for wt, xt in ((qk_lo[a], xT_hi), (qk_hi[a], xT_lo), (qk_hi[a], xT_hi)):
                        last = mm(PR[c % 2][:], wt[:, c % 2, kd], xt[:, kd, half_of(c)],
                                  start=(n == 0), stop=(n == 3 * KD - 1))
                        n += 1
                last.then_inc(proj_done, 1)

            def project_v(pair, c, v):
                if c == 0:
                    pe.wait_ge(vlo_done, pair + 1)
                if c >= 2:
                    pe.wait_ge(v_copied, v - 1)
                elif not (isinstance(v, int) and v < 8):
                    pe.wait_ge(wo_added, v - 5)
                for i in range(2):
                    t = 2 * c + i
                    n = 0
                    for kd in range(KD):
                        for xt, wt in ((xT_hi, v_lo), (xT_lo, v_hi), (xT_hi, v_hi)):
                            last = mm(VO[c % 2][:, i * 256:(i + 1) * 256], xt[:, kd, t * P:(t + 1) * P], wt[:, kd],
                                      start=(n == 0), stop=(n == 3 * KD - 1))
                            n += 1
                last.then_inc(v_done, 1)

            def scores(n, head, a, j):
                if j == 0:
                    pe.wait_ge(rotlo_done, 4 * head + 2)
                if j == 2:
                    pe.wait_ge(rotlo_done, 4 * head + 4)
                if not (isinstance(n, int) and n < 2):
                    pe.wait_ge(exp_done, 2 * n - 2)
                for i in range(2):
                    t = 2 * j + i
                    k0 = max(t - 1, 0)
                    o0 = i * 256 + (k0 - t + 1) * P
                    terms = ((rot_lo(a, 0), rot_hi(a, 1)), (rot_hi(a, 0), rot_lo(a, 1)), (rot_hi(a, 0), rot_hi(a, 1)))
                    for p_, (q, k) in enumerate(terms):
                        last = mm(SC[j % 2][:, o0:(i + 1) * 256], q[:, t * P:(t + 1) * P], k[:, k0 * P:(t + 1) * P],
                                  start=(p_ == 0), stop=(p_ == 2))
                last.then_inc(scores_done, 1)

            def transpose_probs(n, j):
                pe.wait_ge(scaled, n + 1)
                if not (isinstance(n, int) and n == 0):
                    pe.wait_ge(pt_masked, n)
                if isinstance(n, int) and n == LAST - 7:
                    pe.wait_ge(mean_read, 2)
                for i in range(2):
                    last = nc.tensor.transpose(PT[:, i * P:(i + 1) * P], probs[j % 2][:, i], ident_sb[:])
                last.then_inc(pt_done, 1)

            def weigh_v(n, pair, a, j):
                pe.wait_ge(pt_masked, n + 1)
                pe.wait_ge(v_copied, 4 * pair + j + 1)
                if not (isinstance(n, int) and n == 0):
                    pe.wait_ge(otlo_done, n)
                for i in range(2):
                    t = 2 * j + i
                    b0 = 1 if t == 0 else 0
                    for b in range(b0, 2):
                        last = mm(OT[:, i * P:(i + 1) * P], v_sb[:, t - 1 + b, a * HD:(a + 1) * HD],
                                  probsT[:, i, b], start=(b == b0), stop=(b == 1))
                last.then_inc(pv_done, 1)

            def project_out(pair, c, w, last_pair=False):
                if c == 0:
                    pe.wait_ge(olo_done, pair + 1)
                pe.wait_ge(otlo_done, 8 * pair + 5 + c)
                if c >= 2 or last_pair:
                    pe.wait_ge(wo_added, w - 1)
                else:
                    pe.wait_ge(v_copied, w + 7)
                for i in range(2):
                    t = 2 * c + i
                    n = 0
                    for a in range(2):
                        for ot, wt in ((oT_hi(a), o_lo), (oT_lo(a), o_hi), (oT_hi(a), o_hi)):
                            last = mm(VO[c % 2][:, i * 256:(i + 1) * 256], ot[:, t * P:(t + 1) * P], wt[:, a],
                                      start=(n == 0), stop=(n == 5))
                            n += 1
                last.then_inc(wo_done, 1)

            def means_of_abs(n):
                pe.wait_ge(abs_done, 8)
                pe.wait_ge(pt_masked, n)
                mm(PT[:, 0:8], mean_ones[:], abs_sum[:].rearrange("p k i -> p (k i)"),
                   start=True, stop=True).then_inc(mean_done, 1)

            def pair_steps(pair, first, last):
                for s in range(8):
                    n = 8 * pair + s
                    a, j = s // 4, s % 4
                    pa, pj = before(s)
                    if not (first and s == 0):
                        transpose_probs(n - 1, pj)
                    if not (last and s >= 4):
                        project(2 * pair + a + 1, 1 - a, j, n + 4)
                    if 1 <= s <= 4 and not first:
                        project_out(pair - 1, s - 1, 4 * pair - 5 + s)
                    if first and s < 2:
                        project_v(0, s + 2, s + 2)
                    if s == 0 and not first:
                        project_v(pair, 3, 4 * pair + 3)
                    if s >= 5 and not last:
                        project_v(pair + 1, s - 5, 4 * pair + s - 1)
                    if s >= 6 and last:
                        project_out(pair, s - 6, 4 * pair + s - 6, True)
                    early = s % 2 == 0 and not (last and s == 6)
                    if early:
                        scores(n + 1, 2 * pair + (s + 1) // 4, (s + 1) // 4 % 2, (s + 1) % 4)
                    if not (first and s == 0):
                        weigh_v(n - 1, pair if s > 0 else pair - 1, pa, pj)
                    if not early and not (last and s >= 6):
                        scores(n + 1, 2 * pair + (s + 1) // 4, (s + 1) // 4 % 2, (s + 1) % 4)
                    if last and s == 5:
                        scores(n + 2, 2 * pair + 1, 1, 3)
                    if s == 0 and last:
                        means_of_abs(n)

            pe.wait_ge(consts_set, 1)
            warm_up(14)
            pe.wait_ge(ident_in, 16)
            transpose_x(0, 0)
            warm_up(7)
            pe.wait_ge(xt_lo_done, 2)
            project(0, 0, 0, 0)
            project(0, 0, 1, 1)
            transpose_x(0, 1)
            project_v(0, 0, 0)
            pe.wait_ge(xt_lo_done, 4)
            project(0, 0, 2, 2)
            project(0, 0, 3, 3)
            project_v(0, 1, 1)
            scores(0, 0, 0, 0)
            pair_steps(0, True, False)
            with pe.Fori(1, PAIRS - 1) as pair:
                pair_steps(pair, False, False)
            pair_steps(PAIRS - 1, False, True)
            transpose_probs(LAST, 3)
            project_out(PAIRS - 1, 2, 4 * PAIRS - 2, True)
            weigh_v(LAST, PAIRS - 1, 1, 3)
            transpose_x(1, 0)
            project_out(PAIRS - 1, 3, 4 * PAIRS - 1)

            hb = [SC[0], SC[1], VO[0], VO[1]]
            for half in range(2):
                pe.wait_ge(xt_lo_done, 4 + 2 * half + 2)
                for f in range(NF):
                    k = half * NF + f
                    if k in (0, NF // 2):
                        pe.wait_ge(tern_done[0 if k == 0 else 2], 1)
                    if k in (2, 3):
                        pe.wait_ge(wo_added, 4 * PAIRS - 3 + k)
                    if k >= 4:
                        pe.wait_ge(gelu_done, k - 3)
                    for kd in range(KD):
                        for p_, xt in enumerate((xT_lo, xT_hi)):
                            last = mm(hb[k % 4][:], w1_sb[:, kd, f * P:(f + 1) * P],
                                      xt[:, kd, half * HALF:(half + 1) * HALF],
                                      start=(kd == 0 and p_ == 0), stop=(kd == KD - 1 and p_ == 1))
                    last.then_inc(h_done, 1)
                    if k == 5:
                        transpose_x(1, 1)
            yb = [OT, PT, PR[0], PR[1]]
            pe.wait_ge(tern_done[1], 1)
            for c in range(NT // 2):
                pe.wait_ge(glo_done[0], (c // 2 + 1) * NF // 2)
                pe.wait_ge(glo_done[1], (c // 2 + 1) * NF // 2)
                for i in range(2):
                    t = 2 * c + i
                    for f in range(NF):
                        for p_, gt in enumerate((gT_lo, gT_hi)):
                            last = mm(yb[c][:, i * 256:(i + 1) * 256], gt[:, f, t * P:(t + 1) * P], w2_sb[:, f],
                                      start=(f == 0 and p_ == 0), stop=(f == NF - 1 and p_ == 1))
                last.then_inc(y_done, 1)

        @block.scalar
        def _(act):
            copy = nc.scalar.copy

            def xt_hi(ln, half):
                banks = (SC, PR)[ln]
                for kd in range(KD):
                    act.wait_ge(xt_ready, ln * 4 + half * 2 + kd + 1)
                    copy(xT_hi[:, kd, half * HALF:(half + 1) * HALF], banks[kd][:]).then_inc(xt_hi_done, 1)

            def qkhi(a, loads, head, reused):
                act.wait_ge(qk_in[a], 32 * loads)
                if reused:
                    act.wait_ge(proj_done, 4 * (head - 1))
                copy(qk_hi[a][:], qk_raw[a][:]).then_inc(qkhi_done, 1)

            def vhi(pair, reused):
                act.wait_ge(v_in, 16 * (pair + 1))
                if reused:
                    act.wait_ge(v_done, 4 * pair)
                copy(v_hi[:], v_raw[:]).then_inc(vhi_done, 1)

            def ohi(pair, reused):
                act.wait_ge(o_in, 16 * (pair + 1))
                if reused:
                    act.wait_ge(wo_done, 4 * pair)
                copy(o_hi[:], o_raw[:]).then_inc(ohi_done, 1)

            def copy_proj(c, m):
                act.wait_ge(proj_done, m + 1)
                if not (isinstance(m, int) and m < 4):
                    act.wait_ge(rotlo_done, m - 3)
                copy(turn[c][:], PR[c % 2][:]).then_inc(proj_copied, 1)

            def rothi(a, c, m):
                act.wait_ge(rot_done, m + 1)
                copy(rot_hi(a, c % 2)[:, half_of(c)], turn[c][:]).then_inc(rothi_done, 1)

            def exps(n, j):
                act.wait_ge(negmax_done, n + 1)
                for i in range(2):
                    nc.scalar.activation(probs[j % 2][:, i], SC[j % 2][:, i * 256 + P:(i + 1) * 256], ACT.Exp,
                                         bias=negmax[:, j % 2, i:i + 1], scale=SCALE,
                                         accum_out=rowsum[:, j % 2, i:i + 1]).then_inc(exp_done, 1)

            def scale_probs(n, j):
                act.wait_ge(rinv_done, n + 1)
                for i in range(2):
                    last = nc.scalar.activation(probs[j % 2][:, i], probs[j % 2][:, i], ACT.Copy,
                                                scale=rinv[:, j % 2, i:i + 1])
                last.then_inc(scaled, 1)

            def copy_v(c, v):
                act.wait_ge(v_done, v + 1)
                copy(v_sb[:, 2 * c:2 * c + 2], VO[c % 2][:].rearrange("p (t n) -> p t n", t=2)).then_inc(v_copied, 1)

            def ot_hi(n, a, j):
                act.wait_ge(pv_done, n + 1)
                copy(oT_hi(a)[:, 2 * j * P:(2 * j + 2) * P], OT[:, 0:256]).then_inc(othi_done, 1)

            def abs_sums(k, i):
                act.wait_ge(w12_in[k], 16 * (k + 1))
                raw = (w1_raw, w2_raw)[k]
                dest = (w1_sb, w2_sb)[k][:].rearrange("p a b -> p (a b)")
                cs = slice(i * NW // P // 4, (i + 1) * NW // P // 4)
                nc.scalar.activation(dest[:, cs], raw[:, cs], ACT.Abs,
                                     accum_out=abs_sum[:, k, i:i + 1]).then_inc(abs_done, 1)

            def pair_steps(pair, first, last):
                for s in range(8):
                    n = 8 * pair + s
                    m = n + 4
                    a, j = s // 4, s % 4
                    if not (last and s >= 5) and not (first and s == 0):
                        a2, c2 = before(s + 4, 2)
                        rothi(a2, c2, m - 2)
                    exps(n, j)
                    if last and s == 5:
                        rothi(1, 3, m - 2)
                    if first and s == 0:
                        scale_probs(n, j)
                        rothi(0, 2, 2)
                    if not (last and s >= 4):
                        copy_proj(j, m)
                    if not (first and s == 0):
                        scale_probs(n, j)
                        ot_hi(n - 1, *before(s))
                    if s == 0 and not first:
                        copy_v(2, 4 * pair + 2)
                    if s == 1 and not first:
                        copy_v(3, 4 * pair + 3)
                    if s < 2 and first:
                        copy_v(s + 2, s + 2)
                    if s >= 6 and not last:
                        copy_v(s - 6, 4 * pair + s - 2)
                    if s == 1 and not last:
                        qkhi(0, pair + 2, 2 * pair + 2, True)
                    if s == 5 and not last:
                        qkhi(1, pair + 2, 2 * pair + 3, True)
                    if s == 3 and not last:
                        vhi(pair + 1, True)
                    if s == (4 if last else 6):
                        ohi(pair, not first)
                    if first:
                        abs_sums(s // 4, s % 4)

            nc.scalar.preload_act_table(ACT.Exp)
            qkhi(0, 1, 0, False)
            vhi(0, False)
            xt_hi(0, 0)
            qkhi(1, 1, 1, False)
            copy_proj(0, 0)
            copy_proj(1, 1)
            xt_hi(0, 1)
            copy_v(0, 0)
            rothi(0, 0, 0)
            copy_proj(2, 2)
            rothi(0, 1, 1)
            copy_proj(3, 3)
            copy_v(1, 1)
            pair_steps(0, True, False)
            with act.Fori(1, PAIRS - 1) as pair:
                pair_steps(pair, False, False)
            pair_steps(PAIRS - 1, False, True)
            nc.scalar.preload_act_table(ACT.Gelu)
            ot_hi(LAST, 1, 3)
            xt_hi(1, 0)
            act.wait_ge(bias_in, 32)
            hb = [SC[0], SC[1], VO[0], VO[1]]
            for k in range(2 * NF):
                f = k % NF
                act.wait_ge(h_done, k + 1)
                if k >= 4:
                    by, count = lo_by(k - 4)
                    act.wait_ge(glo_done[by], count)
                nc.scalar.activation(gelu_tmp[k % 4][:], hb[k % 4][:], ACT.Gelu,
                                     bias=b1_sb[:, f:f + 1]).then_inc(gelu_done, 1)
                if k % 4 == 3:
                    hs = slice((k // NF) * HALF, (k // NF + 1) * HALF)
                    act.wait_ge(gelu_done, k + 1)
                    copy(gT_hi[:, f, hs], gelu_tmp[k % 4][:]).then_inc(ghi_done[1], 1)
                if k == 5:
                    xt_hi(1, 1)

        @block.vector
        def _(dve):
            tt = nc.vector.tensor_tensor

            def norm_stats(ln, half):
                hs = slice(half * 4, half * 4 + 4)
                for t in range(half * 4, half * 4 + 4):
                    if ln == 0 and t % 2 == 0:
                        dve.wait_ge(x_in[t // 2], 16)
                    if ln == 1 and t % 2 == 0:
                        dve.wait_ge(wo_added, 4 * PAIRS - 3 + t // 2)
                    nc.vector.bn_stats(stats[:, t], xres[:, t]).then_inc(bn_done, 1)
                for t in range(half * 4, half * 4 + 4):
                    dve.wait_ge(bn_done, ln * NT + t + 1)
                    nc.vector.bn_aggr(mv[:, t], stats[:, t]).then_inc(aggr_done, 1)
                dve.wait_ge(aggr_done, ln * NT + half * 4 + 4)
                nc.vector.tensor_scalar(var_eps[:, hs], mv[:, hs, 1], EPS_LN, None, ALU.add).then_inc(var_ready, 1)

            def normalise(ln, half):
                dve.wait_ge(rstd_ready, 2 * ln + half + 1)
                for t in range(half * 4, half * 4 + 4):
                    nc.vector.tensor_scalar(xnorm[:, t], xres[:, t], mv[:, t, 0:1], rstd[:, t:t + 1],
                                            ALU.subtract, ALU.mult).then_inc(xn_ready, 1)

            def xt_lo(ln, half):
                banks = (SC, PR)[ln]
                hs = slice(half * HALF, (half + 1) * HALF)
                for kd in range(KD):
                    dve.wait_ge(xt_hi_done, ln * 4 + half * 2 + kd + 1)
                    tt(xT_lo[:, kd, hs], banks[kd][:], xT_hi[:, kd, hs].bitcast(F32),
                       ALU.subtract).then_inc(xt_lo_done, 1)

            def times_cos(c, m, swaps):
                dve.wait_ge(swap_in[c], 32 * swaps)
                tt(turn[c][:], turn[c][:], cos_sb[:, half_of(c)], ALU.mult).then_inc(cos_done, 1)

            def early_cos(c):
                if c == 0:
                    dve.wait_ge(tab_in[0], 32)
                dve.wait_ge(proj_copied, c + 1)
                tt(cos_product[:, c * HALF:(c + 1) * HALF], turn[c][:], cos_sb[:, half_of(c)],
                   ALU.mult).then_inc(cos_done, 1)

            def rotate(c):
                if c == 3:
                    dve.wait_ge(rot_done, 3)
                if c < 2:
                    product = cos_product[:, c * HALF:(c + 1) * HALF]
                    dve.wait_ge(cos_done, c + 1)
                    dve.wait_ge(swap_in[c], 32)
                else:
                    product = turn[c][:]
                    times_cos(c, c, 1)
                tt(swapped[c][:], swapped[c][:], sin_sb[:, half_of(c)], ALU.mult).then_inc(sin_done, 1)
                dve.wait_ge(sin_done, c + 1)
                tt(turn[c][:], product, swapped[c][:], ALU.add).then_inc(rot_done, 1)

            def rotlo(a, c, m):
                dve.wait_ge(rothi_done, m + 1)
                tt(rot_lo(a, c % 2)[:, half_of(c)], turn[c][:], rot_hi(a, c % 2)[:, half_of(c)].bitcast(F32),
                   ALU.subtract).then_inc(rotlo_done, 1)

            def merge(n, j, first_in_loop):
                if first_in_loop:
                    dve.wait_ge(scores_done, n + 1)
                    nc.vector.memset(rowsum[:, j % 2], 0.0)
                else:
                    dve.wait_ge(mask_in, 32)
                    dve.wait_ge(scores_done, n + 1)
                sc = SC[j % 2][:].rearrange("p (i b k) -> p i b k", i=2, b=2)
                if j == 0:
                    nc.vector.copy_predicated(sc[:, 0, 1], in_prev_sb[:], nothing[:])
                    nc.vector.copy_predicated(sc[:, 1, 1], in_prev_sb[:], sc[:, 1, 0]).then_inc(merged, 1)
                else:
                    nc.vector.copy_predicated(sc[:, :, 1], in_prev_sb[:].unsqueeze(1).broadcast_to([P, 2, P]),
                                              sc[:, :, 0]).then_inc(merged, 1)
                dve.wait_ge(merged, n + 1)
                nc.vector.tensor_reduce(rowmax[:, j % 2], sc[:, :, 1], AX.X, ALU.max).then_inc(max_done, 1)
                dve.wait_ge(max_done, n + 1)
                nc.vector.tensor_scalar(negmax[:, j % 2], rowmax[:, j % 2], -SCALE, None,
                                        ALU.mult).then_inc(negmax_done, 1)

            def inverse_sum(n, j):
                dve.wait_ge(exp_done, 2 * n + 2)
                nc.vector.reciprocal(rinv[:, j % 2], rowsum[:, j % 2]).then_inc(rinv_done, 1)

            def mask_pt(n):
                dve.wait_ge(pt_done, n + 1)
                if not (isinstance(n, int) and n == 0):
                    dve.wait_ge(pv_done, n)
                tt(probsT[:], PT[:, 0:256].rearrange("p (i q) -> p i q", i=2).unsqueeze(2).broadcast_to([P, 2, 2, P]),
                   mask_sb[:].unsqueeze(1).broadcast_to([P, 2, 2, P]), ALU.mult).then_inc(pt_masked, 1)

            def ot_lo(n, a, j):
                dve.wait_ge(othi_done, n + 1)
                ts = slice(2 * j * P, (2 * j + 2) * P)
                tt(oT_lo(a)[:, ts], OT[:, 0:256], oT_hi(a)[:, ts].bitcast(F32), ALU.subtract).then_inc(otlo_done, 1)

            def add_out(c, w):
                dve.wait_ge(wo_done, w + 1)
                ts = slice(2 * c, 2 * c + 2)
                tt(xres[:, ts], VO[c % 2][:].rearrange("p (t d) -> p t d", t=2), xres[:, ts], ALU.add).then_inc(wo_added, 1)

            def thresholds():
                dve.wait_ge(mean_done, 1)
                for k in range(2):
                    nc.vector.tensor_reduce(mean_abs[:, k:k + 1], PT[:, 4 * k:4 * k + 4], AX.X,
                                            ALU.add).then_inc(mean_read, 1)
                dve.wait_ge(mean_read, 2)
                nc.vector.tensor_scalar(thr[:, :, 0], mean_abs[:], EPS_Q, 0.5, ALU.max, ALU.mult)
                nc.vector.tensor_scalar(thr[:, :, 1], mean_abs[:], EPS_Q, -0.5, ALU.max, ALU.mult).then_inc(thr_done, 1)

            def ternary_w1():
                raw = w1_raw[:].rearrange("p (k f) -> p k f", k=KD)[:, :, F // 2:]
                dest = w1_sb[:, :, F // 2:]
                dve.wait_ge(thr_done, 1)
                nc.vector.tensor_scalar(dest, raw, thr[:, 0, 1:2], None, ALU.is_lt).then_inc(below_done[2], 1)
                dve.wait_ge(below_done[2], 1)
                nc.vector.scalar_tensor_tensor(dest, raw, thr[:, 0, 0:1], dest.bitcast(F32), ALU.is_gt,
                                               ALU.subtract).then_inc(tern_done[2], 1)

            def ternary_w2():
                dest = w2_sb[:].rearrange("p a b -> p (a b)")
                dve.wait_ge(below_done[1], 1)
                nc.vector.scalar_tensor_tensor(dest, w2_raw[:], thr[:, 1, 0:1], dest.bitcast(F32), ALU.is_gt,
                                               ALU.subtract).then_inc(tern_done[1], 1)

            def pair_steps(pair, first, last):
                for s in range(8):
                    n = 8 * pair + s
                    m = n + 4
                    j = s % 4
                    merge(n, j, s < 2 and not isinstance(n, int))
                    if not (first and s == 0):
                        mask_pt(n - 1)
                    if s == 7 and last:
                        add_out(0, 4 * pair)
                    if first and s == 0:
                        inverse_sum(n, j)
                        rotate(3)
                        rotlo(0, 2, 2)
                    elif last and s == 5:
                        inverse_sum(n, j)
                        rotlo(1, 3, m - 2)
                    else:
                        if not (last and s >= 6):
                            rotlo(*before(s + 4, 2), m - 2)
                        inverse_sum(n, j)
                    if s == 6 and last:
                        ternary_w1()
                    if not (last and s >= 5) and not (first and s == 0):
                        c1 = (s - 1) % 4
                        times_cos(c1, m - 1, 2 * pair + (s + 3) // 4 + 1)
                    if 1 <= s <= 4 and not first:
                        add_out(s - 1, 4 * pair - 5 + s)
                    if not (first and s == 0):
                        ot_lo(n - 1, *before(s))
                    if s == 0 and last:
                        thresholds()
                    if s == 7 and last:
                        add_out(1, 4 * pair + 1)

            nc.vector.memset(mean_ones[:], 1.0 / NW)
            nc.vector.memset(minus_half[:], -0.5).then_inc(consts_set, 1)
            norm_stats(0, 0)
            normalise(0, 0)
            xt_lo(0, 0)
            norm_stats(0, 1)
            early_cos(0)
            normalise(0, 1)
            early_cos(1)
            xt_lo(0, 1)
            rotate(0)
            rotate(1)
            rotlo(0, 0, 0)
            rotlo(0, 1, 1)
            dve.wait_ge(tab_in[1], 32)
            times_cos(2, 2, 1)
            dve.wait_ge(nothing_set, 1)
            dve.wait_ge(mask_in, 32)
            pair_steps(0, True, False)
            with dve.Fori(1, PAIRS - 1) as pair:
                pair_steps(pair, False, False)
            pair_steps(PAIRS - 1, False, True)
            norm_stats(1, 0)
            mask_pt(LAST)
            add_out(2, 4 * PAIRS - 2)
            normalise(1, 0)
            ot_lo(LAST, 1, 3)
            xt_lo(1, 0)
            add_out(3, 4 * PAIRS - 1)
            norm_stats(1, 1)

            def ghi(k):
                hs = slice((k // NF) * HALF, (k // NF + 1) * HALF)
                dve.wait_ge(gelu_done, k + 1)
                nc.vector.tensor_copy(gT_hi[:, k % NF, hs], gelu_tmp[k % 4][:]).then_inc(ghi_done[0], 1)

            def glo(k):
                hs = slice((k // NF) * HALF, (k // NF + 1) * HALF)
                by, count = hi_by(k)
                dve.wait_ge(ghi_done[by], count)
                tt(gT_lo[:, k % NF, hs], gelu_tmp[k % 4][:], gT_hi[:, k % NF, hs].bitcast(F32),
                   ALU.subtract).then_inc(glo_done[0], 1)

            ghi(0)
            normalise(1, 1)
            for k in range(2 * NF):
                if (k + 1) % 4 != 3 and k + 1 < 2 * NF:
                    ghi(k + 1)
                if k % 2 == 0:
                    glo(k)
                if k == 4:
                    xt_lo(1, 1)
                if k == 8:
                    ternary_w2()
            yb = [OT, PT, PR[0], PR[1]]
            dve.wait_ge(b2_added, NT)
            for c in range(NT // 2):
                dve.wait_ge(y_done, c + 1)
                tt(final[:, 2 * c:2 * c + 2], yb[c][:].rearrange("p (t d) -> p t d", t=2), xres[:, 2 * c:2 * c + 2],
                   ALU.add).then_inc(fin_done, 1)

        @block.gpsimd
        def _(pool):
            tt = nc.gpsimd.tensor_tensor

            def rsqrt(ln, half):
                hs = slice(half * 4, half * 4 + 4)
                pool.wait_ge(var_ready, 2 * ln + half + 1)
                tt(rstd[:, hs], var_eps[:, hs], minus_half[:, hs], ALU.pow).then_inc(rstd_ready, 1)

            def qklo(a, head):
                pool.wait_ge(qkhi_done, head + 1)
                tt(qk_lo[a][:], qk_raw[a][:], qk_hi[a][:].bitcast(F32), ALU.subtract).then_inc(qklo_done, 1)

            def vlo(pair):
                pool.wait_ge(vhi_done, pair + 1)
                tt(v_lo[:], v_raw[:], v_hi[:].bitcast(F32), ALU.subtract).then_inc(vlo_done, 1)

            def olo(pair):
                pool.wait_ge(ohi_done, pair + 1)
                tt(o_lo[:], o_raw[:], o_hi[:].bitcast(F32), ALU.subtract).then_inc(olo_done, 1)

            def rotate(c, m, swaps):
                pool.wait_ge(swap_in[c], 32 * swaps)
                tt(swapped[c][:], swapped[c][:], sin_sb[:, half_of(c)], ALU.mult).then_inc(sin_done, 1)
                pool.wait_ge(cos_done, m + 1)
                pool.wait_ge(sin_done, m + 1)
                tt(turn[c][:], turn[c][:], swapped[c][:], ALU.add).then_inc(rot_done, 1)

            def ternary_w1(step):
                raw = w1_raw[:].rearrange("p (k f) -> p k f", k=KD)[:, :, :F // 2]
                dest = w1_sb[:, :, :F // 2]
                kd = step % KD
                if step == 0:
                    pool.wait_ge(thr_done, 1)
                if step < KD:
                    nc.gpsimd.tensor_scalar(dest[:, kd], raw[:, kd], thr[:, 0, 1:2], None,
                                            ALU.is_lt).then_inc(below_done[0], 1)
                elif step < 2 * KD:
                    nc.gpsimd.tensor_scalar(raw[:, kd], raw[:, kd], thr[:, 0, 0:1], None,
                                            ALU.is_gt).then_inc(above_done, 1)
                else:
                    pool.wait_ge(below_done[0], KD)
                    pool.wait_ge(above_done, KD)
                    tt(dest, raw, dest.bitcast(F32), ALU.subtract).then_inc(tern_done[0], 1)

            def below_w2():
                dest = w2_sb[:].rearrange("p a b -> p (a b)")
                nc.gpsimd.tensor_scalar(dest, w2_raw[:], thr[:, 1, 1:2], None, ALU.is_lt).then_inc(below_done[1], 1)

            def pair_steps(pair, first, last):
                for s in range(8):
                    m = 8 * pair + s + 4
                    if first and s == 1:
                        pool.wait_ge(rot_done, 4)
                    if not (last and s >= 5) and not (first and s == 0):
                        rotate((s - 1) % 4, m - 1, 2 * pair + (s + 3) // 4 + 1)
                    if s == 1 and not last:
                        qklo(0, 2 * pair + 2)
                    if s == 5 and not last:
                        qklo(1, 2 * pair + 3)
                    if s == 3 and not last:
                        vlo(pair + 1)
                    if s == (4 if last else 6):
                        olo(pair)
                    if last and 1 <= s <= 4:
                        ternary_w1(s - 1)

            nc.gpsimd.memset(nothing[:], -BIG).then_inc(nothing_set, 1)
            pool.wait_ge(consts_set, 1)
            rsqrt(0, 0)
            qklo(0, 0)
            rsqrt(0, 1)
            vlo(0)
            qklo(1, 1)
            pool.wait_ge(tab_in[1], 32)
            pool.wait_ge(rot_done, 2)
            rotate(2, 2, 1)
            pair_steps(0, True, False)
            with pool.Fori(1, PAIRS - 1) as pair:
                pair_steps(pair, False, False)
            pair_steps(PAIRS - 1, False, True)
            ternary_w1(2 * KD)
            below_w2()
            rsqrt(1, 0)
            rsqrt(1, 1)
            pool.wait_ge(bias_in, 32)
            for k in range(2 * NF):
                hs = slice((k // NF) * HALF, (k // NF + 1) * HALF)
                if k % 2 == 1:
                    by, count = hi_by(k)
                    pool.wait_ge(ghi_done[by], count)
                    tt(gT_lo[:, k % NF, hs], gelu_tmp[k % 4][:], gT_hi[:, k % NF, hs].bitcast(F32),
                       ALU.subtract).then_inc(glo_done[1], 1)
                if k % 2 == 0:
                    t = k // 2
                    pool.wait_ge(xn_ready, NT + t + 1)
                    tt(xres[:, t], xres[:, t], b2_sb[:], ALU.add).then_inc(b2_added, 1)


def tables(T, HD):
    import numpy as np
    inv_freq = (np.float32(1.0) / np.power(np.float32(10000.0), np.arange(0, HD, 2, dtype=np.float32) / np.float32(HD))).astype(np.float32)
    freqs = np.arange(T, dtype=np.float32)[:, None] * inv_freq[None, :]
    c, s = np.cos(freqs).astype(np.float32).T, np.sin(freqs).astype(np.float32).T
    q = np.arange(HD)[:, None]
    k = np.arange(HD)[None, :]
    prev = k > q
    mask_t = np.concatenate([prev.T, ~prev.T], 1)
    return {"cos_t": np.concatenate([c, c], 0), "sin_t": np.concatenate([-s, s], 0),
            "in_prev": prev.astype(np.int32), "mask_t": mask_t.astype(np.float32), "ident": np.eye(HD, dtype=np.float32)}


def kernel(L0_attn_hidden_states, L0_attn_wq, L0_attn_wk, L0_attn_wv, L0_attn_wo, L0_ffn_w1, L0_ffn_b1, L0_ffn_w2,
           L0_ffn_b2):
    import numpy as np
    import concourse.bacc as bacc
    from concourse.bass_utils import run_bass_kernel_spmd as run

    x = np.asarray(L0_attn_hidden_states)
    arrays = {"x": x[0], "wq": L0_attn_wq, "wk": L0_attn_wk, "wv": L0_attn_wv, "wo": L0_attn_wo,
              "w1t": np.asarray(L0_ffn_w1).T, "b1": np.asarray(L0_ffn_b1).reshape(-1, P).T, "w2t": np.asarray(L0_ffn_w2).T, "b2": L0_ffn_b2,
              **tables(x.shape[1], P)}
    arrays = {k: np.ascontiguousarray(v) for k, v in arrays.items()}
    nc = bacc.Bacc("TRN2", target_bir_lowering=False, num_devices=1)
    args = {k: nc.dram_tensor(f"in_{k}", v.shape, mybir.dt.from_np(v.dtype), kind="ExternalInput").ap()
            for k, v in arrays.items()}
    out = nc.dram_tensor("out_y", x[0].shape, F32, kind="ExternalOutput").ap()
    preln_block_kernel(nc, out=out, **args)
    r = run(nc, [{f"in_{k}": v for k, v in arrays.items()}], core_ids=[0])
    return r.results[0]["out_y"].reshape(x.shape)
```

```python
from contextlib import ExitStack

import concourse.bass as bass
from concourse import mybir

P = 128
ALU = mybir.AluOpType
ACT = mybir.ActivationFunctionType
AX = mybir.AxisListType
F32 = mybir.dt.float32
F32R = mybir.dt.float32r
BIG = 3.4028234663852886e38


def preln_block_kernel(nc, x, wq, wk, wv, wo, w1t, b1, w2t, b2, cos_t, sin_t, in_prev, mask_t, ident, out):
    T, D = x.shape
    HD = P
    HEADS = wq.shape[1] // HD
    PAIRS = HEADS // 2
    NT = T // P
    KD = D // P
    F = w1t.shape[1]
    NF = F // P
    HALF = T // 2
    SCALE = float(HD) ** -0.5
    EPS_LN = 1e-5
    EPS_Q = 1e-8
    NW = D * F
    CHUNKS = 4 * HEADS
    LAST = 8 * PAIRS - 1
    assert T == 1024 and D == 256 and F == 1024

    with ExitStack() as ctx:
        def sb(name, shape, dt=F32):
            return ctx.enter_context(nc.sbuf_tensor(name, shape, dt))

        def bank(name):
            return ctx.enter_context(nc.psum_tensor(name, [P, 512], F32))

        def sem(name):
            return ctx.enter_context(nc.semaphore(name))

        xres = sb("xres", [P, NT, D])
        xnorm = sb("xnorm", [P, NT, D])
        xT_hi = sb("xT_hi", [P, KD, T], F32R)
        xT_lo = sb("xT_lo", [P, KD, T], F32R)
        qk_raw = [sb(f"qk_raw{a}", [P, 2, KD, HD]) for a in range(2)]
        qk_hi = [sb(f"qk_hi{a}", [P, 2, KD, HD], F32R) for a in range(2)]
        qk_lo = [sb(f"qk_lo{a}", [P, 2, KD, HD], F32R) for a in range(2)]
        v_raw = sb("v_raw", [P, KD, 2 * HD])
        v_hi = sb("v_hi", [P, KD, 2 * HD], F32R)
        v_lo = sb("v_lo", [P, KD, 2 * HD], F32R)
        o_raw = sb("o_raw", [P, 2, D])
        o_hi = sb("o_hi", [P, 2, D], F32R)
        o_lo = sb("o_lo", [P, 2, D], F32R)
        turn = [sb(f"turn{c}", [P, 512]) for c in range(4)]
        swapped = [sb(f"swapped{c}", [P, 512]) for c in range(4)]
        cos_sb = sb("cos_sb", [P, T])
        sin_sb = sb("sin_sb", [P, T])
        in_prev_sb = sb("in_prev_sb", [P, P], mybir.dt.int32)
        mask_sb = sb("mask_sb", [P, 2, P])
        nothing = sb("nothing", [P, P])
        ident_sb = sb("ident_sb", [P, P])
        probs = [sb(f"probs{i}", [P, 2, P]) for i in range(2)]
        rowmax = sb("rowmax", [P, 2, 2])
        negmax = sb("negmax", [P, 2, 2])
        rowsum = sb("rowsum", [P, 2, 2])
        rinv = sb("rinv", [P, 2, 2])
        probsT = sb("probsT", [P, 2, 2, P])
        v_sb = sb("v_sb", [P, NT, 2 * HD])
        gT_hi = sb("gT_hi", [P, NF, T], F32R)
        gT_lo = sb("gT_lo", [P, NF, T], F32R)

        def rot_hi(a, w):
            return gT_hi[:, 2 * a + w]

        def rot_lo(a, w):
            return gT_lo[:, 2 * a + w]

        def oT_hi(a):
            return gT_hi[:, 4 + a]

        def oT_lo(a):
            return gT_lo[:, 4 + a]

        w1_raw = sb("w1_raw", [P, KD * F])
        w2_raw = sb("w2_raw", [P, NF * D])
        cos_product = w2_raw
        w1_sb = sb("w1_sb", [P, KD, F], F32R)
        w2_sb = sb("w2_sb", [P, NF, D], F32R)
        b1_sb = sb("b1_sb", [P, NF])
        b2_sb = sb("b2_sb", [P, D])
        stats = sb("stats", [P, NT, 6])
        mv = sb("mv", [P, NT, 2])
        rstd = sb("rstd", [P, NT])
        var_eps = sb("var_eps", [P, NT])
        minus_half = sb("minus_half", [P, NT])
        mean_ones = sb("mean_ones", [P, P])
        abs_sum = sb("abs_sum", [P, 2, 4])
        mean_abs = sb("mean_abs", [P, 2])
        thr = sb("thr", [P, 2, 2])
        gelu_tmp = turn
        final = xnorm

        PR = [bank(f"PR{i}") for i in range(2)]
        SC = [bank(f"SC{i}") for i in range(2)]
        PT = bank("PT")
        OT = bank("OT")
        VO = [bank(f"VO{i}") for i in range(2)]

        x_in = [sem(f"x_in{i}") for i in range(4)]
        tab_in = [sem(f"tab_in{i}") for i in range(2)]
        mask_in = sem("mask_in")
        ident_in = sem("ident_in")
        bias_in = sem("bias_in")
        w12_in = [sem(f"w{k + 1}_in") for k in range(2)]
        qk_in = [sem(f"qk_in{a}") for a in range(2)]
        v_in = sem("v_in")
        o_in = sem("o_in")
        swap_in = [sem(f"swap_in{c}") for c in range(4)]
        consts_set = sem("consts_set")
        nothing_set = sem("nothing_set")
        bn_done = sem("bn_done")
        aggr_done = sem("aggr_done")
        var_ready = sem("var_ready")
        rstd_ready = sem("rstd_ready")
        xn_ready = sem("xn_ready")
        xt_ready = sem("xt_ready")
        xt_hi_done = sem("xt_hi_done")
        xt_lo_done = sem("xt_lo_done")
        qkhi_done = sem("qkhi_done")
        qklo_done = sem("qklo_done")
        vhi_done = sem("vhi_done")
        vlo_done = sem("vlo_done")
        ohi_done = sem("ohi_done")
        olo_done = sem("olo_done")
        proj_done = sem("proj_done")
        proj_copied = sem("proj_copied")
        cos_done = sem("cos_done")
        sin_done = sem("sin_done")
        rot_done = sem("rot_done")
        rothi_done = sem("rothi_done")
        rotlo_done = sem("rotlo_done")
        scores_done = sem("scores_done")
        merged = sem("merged")
        max_done = sem("max_done")
        negmax_done = sem("negmax_done")
        exp_done = sem("exp_done")
        rinv_done = sem("rinv_done")
        scaled = sem("scaled")
        pt_done = sem("pt_done")
        pt_masked = sem("pt_masked")
        pv_done = sem("pv_done")
        othi_done = sem("othi_done")
        otlo_done = sem("otlo_done")
        v_done = sem("v_done")
        v_copied = sem("v_copied")
        wo_done = sem("wo_done")
        wo_added = sem("wo_added")
        abs_done = sem("abs_done")
        mean_done = sem("mean_done")
        mean_read = sem("mean_read")
        thr_done = sem("thr_done")
        below_done = [sem("w1_below_a"), sem("w2_below"), sem("w1_below_b")]
        above_done = sem("w1_above_a")
        tern_done = [sem("w1_ternary_a"), sem("w2_ternary"), sem("w1_ternary_b")]
        h_done = sem("h_done")
        gelu_done = sem("gelu_done")
        ghi_done = [sem("ghi_dve"), sem("ghi_act")]
        glo_done = [sem("glo_dve"), sem("glo_pool")]
        b2_added = sem("b2_added")
        y_done = sem("y_done")
        fin_done = sem("fin_done")
        out_done = sem("out_done")

        def half_of(c):
            return slice((c // 2) * HALF, (c // 2 + 1) * HALF)

        def before(s, d=1):
            return ((s - d) % 8) // 4, (s - d) % 4

        def hi_by(k):
            return (1, k // 4 + 1) if k % 4 == 3 else (0, k - k // 4 + 1)

        def lo_by(k):
            return k % 2, k // 2 + 1

        LAST_STEPS = 4


        block = ctx.enter_context(nc.Block())

        @block.sync
        def _(sp):
            xv = x.rearrange("(t p) d -> p t d", p=P)
            ov = out.rearrange("(t p) d -> p t d", p=P)

            def load_head(head, a):
                for w, src in ((0, wq), (1, wk)):
                    s = src.rearrange("(k p) n -> p k n", p=P)
                    sp.dma_start(qk_raw[a][:, w], s[:, :, bass.ds(head * HD, HD)]).then_inc(qk_in[a], 16)

            def load_v(pair):
                s = wv.rearrange("(k p) n -> p k n", p=P)
                sp.dma_start(v_raw[:], s[:, :, bass.ds(pair * 2 * HD, 2 * HD)]).then_inc(v_in, 16)

            def load_o(pair):
                s = wo[bass.ds(pair * 2 * HD, 2 * HD), :].rearrange("(a p) n -> p a n", p=P)
                sp.dma_start(o_raw[:], s).then_inc(o_in, 16)

            def load_tables(half):
                hs = slice(half * HALF, (half + 1) * HALF)
                sp.dma_start(cos_sb[:, hs], cos_t[:, hs]).then_inc(tab_in[half], 16)
                sp.dma_start(sin_sb[:, hs], sin_t[:, hs]).then_inc(tab_in[half], 16)

            def swap(m, c):
                sp.wait_ge(proj_copied, m + 1)
                for to, fr in ((0, HD // 2), (HD // 2, 0)):
                    sp.dma_start(swapped[c][to:to + HD // 2, :],
                                 turn[c][fr:fr + HD // 2, :]).then_inc(swap_in[c], 16)

            def pair_steps(pair, ahead, first=False):
                for s in range(8):
                    if not (ahead == 0 and s >= 4):
                        swap(8 * pair + s + 4, s % 4)
                    if first and s in (1, 2):
                        sp.wait_ge(rot_done, 2)
                        h = NF // 2
                        fs = slice((s - 1) * h, s * h)
                        sp.dma_start(w2_raw[:].rearrange("p (f n) -> p f n", f=NF)[:, fs],
                                     w2t.rearrange("(f p) n -> p f n", p=P)[:, fs]).then_inc(w12_in[1], 16)
                    if s == 2 and ahead == 2:
                        sp.wait_ge(qklo_done, 2 * pair + 3)
                        load_head(2 * pair + 4, 0)
                    if s == 6 and ahead == 2:
                        sp.wait_ge(qklo_done, 2 * pair + 4)
                        load_head(2 * pair + 5, 1)
                    if s == 4 and ahead == 2:
                        sp.wait_ge(vlo_done, pair + 2)
                        load_v(pair + 2)
                    if s == 7 and ahead >= 1:
                        sp.wait_ge(olo_done, pair + 1)
                        load_o(pair + 1)

            for i in range(4):
                sp.dma_start(xres[:, 2 * i:2 * i + 2], xv[:, 2 * i:2 * i + 2]).then_inc(x_in[i], 16)
                if i == 1:
                    load_head(0, 0)
                    sp.dma_start(ident_sb[:], ident).then_inc(ident_in, 16)
            load_v(0)
            load_tables(0)
            load_head(1, 1)
            sp.dma_start(in_prev_sb[:], in_prev).then_inc(mask_in, 16)
            sp.dma_start(mask_sb[:].rearrange("p b q -> p (b q)"), mask_t).then_inc(mask_in, 16)
            load_tables(1)
            sp.wait_ge(qklo_done, 1)
            load_head(2, 0)
            swap(0, 0)
            swap(1, 1)
            sp.dma_start(w1_raw[:].rearrange("p (k f) -> p k f", k=KD),
                         w1t.rearrange("(k p) f -> p k f", p=P)).then_inc(w12_in[0], 16)
            sp.wait_ge(vlo_done, 1)
            load_v(1)
            load_o(0)
            swap(2, 2)
            swap(3, 3)
            sp.wait_ge(qklo_done, 2)
            load_head(3, 1)
            sp.dma_start(b1_sb[:], b1).then_inc(bias_in, 16)
            sp.dma_start(b2_sb[:], b2.rearrange("(a d) -> a d", a=1).broadcast_to([P, D])).then_inc(bias_in, 16)
            pair_steps(0, 2, True)
            with sp.Fori(1, PAIRS - 2) as pair:
                pair_steps(pair, 2)
            pair_steps(PAIRS - 2, 1)
            pair_steps(PAIRS - 1, 0)
            pieces = [(0, 2), (2, 4), (4, 6), (6, 7), (7, 8)]
            for i, (t0, t1) in enumerate(pieces):
                sp.wait_ge(fin_done, i + 1)
                sp.dma_start(ov[:, t0:t1], final[:, t0:t1]).then_inc(out_done, 16)
            sp.wait_ge(out_done, 16 * len(pieces))

        @block.tensor
        def _(pe):
            mm = nc.tensor.matmul

            def transpose_x(ln, half):
                banks = (SC, PR)[ln]
                if half == 1:
                    pe.wait_ge(xt_lo_done, ln * 4 + 2)
                for t in range(4):
                    pe.wait_ge(xn_ready, ln * NT + half * 4 + t + 1)
                    for kd in range(KD):
                        tr = nc.tensor.transpose(banks[kd][:, t * P:(t + 1) * P],
                                                 xnorm[:, half * 4 + t, kd * P:(kd + 1) * P], ident_sb[:])
                        if t == 3:
                            tr.then_inc(xt_ready, 1)

            def keep_warm(bank, products):
                for _ in range(products):
                    mm(bank[:, 0:P], mean_ones[:], mean_ones[:], start=True, stop=True)

            def project(head, a, c, m, split=None):
                if c == 0:
                    pe.wait_ge(qklo_done, head + 1)
                if not (isinstance(m, int) and m < 2):
                    pe.wait_ge(proj_copied, m - 1)
                n = 0
                for kd in range(KD):
                    if split is not None:
                        pe.wait_ge(xt_lo_done, split + kd + 1)
                    for wt, xt in ((qk_lo[a], xT_hi), (qk_hi[a], xT_lo), (qk_hi[a], xT_hi)):
                        last = mm(PR[c % 2][:], wt[:, c % 2, kd], xt[:, kd, half_of(c)],
                                  start=(n == 0), stop=(n == 3 * KD - 1))
                        n += 1
                last.then_inc(proj_done, 1)

            def project_v(pair, c, v):
                if c == 0:
                    pe.wait_ge(vlo_done, pair + 1)
                if c >= 2:
                    pe.wait_ge(v_copied, v - 1)
                elif not (isinstance(v, int) and v < 8):
                    pe.wait_ge(wo_added, v - 5)
                for i in range(2):
                    t = 2 * c + i
                    n = 0
                    for kd in range(KD):
                        for xt, wt in ((xT_hi, v_lo), (xT_lo, v_hi), (xT_hi, v_hi)):
                            last = mm(VO[c % 2][:, i * 256:(i + 1) * 256], xt[:, kd, t * P:(t + 1) * P], wt[:, kd],
                                      start=(n == 0), stop=(n == 3 * KD - 1))
                            n += 1
                last.then_inc(v_done, 1)

            def scores(n, head, a, j):
                if j == 0:
                    pe.wait_ge(rotlo_done, 4 * head + 2)
                if j == 2:
                    pe.wait_ge(rotlo_done, 4 * head + 4)
                if not (isinstance(n, int) and n < 2):
                    pe.wait_ge(exp_done, 2 * n - 2)
                for i in range(2):
                    t = 2 * j + i
                    k0 = max(t - 1, 0)
                    o0 = i * 256 + (k0 - t + 1) * P
                    terms = ((rot_lo(a, 0), rot_hi(a, 1)), (rot_hi(a, 0), rot_lo(a, 1)), (rot_hi(a, 0), rot_hi(a, 1)))
                    for p_, (q, k) in enumerate(terms):
                        last = mm(SC[j % 2][:, o0:(i + 1) * 256], q[:, t * P:(t + 1) * P], k[:, k0 * P:(t + 1) * P],
                                  start=(p_ == 0), stop=(p_ == 2))
                last.then_inc(scores_done, 1)

            def transpose_probs(n, j):
                pe.wait_ge(scaled, n + 1)
                if not (isinstance(n, int) and n == 0):
                    pe.wait_ge(pt_masked, n)
                for i in range(2):
                    last = nc.tensor.transpose(PT[:, i * P:(i + 1) * P], probs[j % 2][:, i], ident_sb[:])
                last.then_inc(pt_done, 1)

            def weigh_v(n, pair, a, j):
                pe.wait_ge(pt_masked, n + 1)
                pe.wait_ge(v_copied, 4 * pair + j + 1)
                if not (isinstance(n, int) and n == 0):
                    pe.wait_ge(otlo_done, n)
                for i in range(2):
                    t = 2 * j + i
                    b0 = 1 if t == 0 else 0
                    for b in range(b0, 2):
                        last = mm(OT[:, i * P:(i + 1) * P], v_sb[:, t - 1 + b, a * HD:(a + 1) * HD],
                                  probsT[:, i, b], start=(b == b0), stop=(b == 1))
                last.then_inc(pv_done, 1)

            def project_out(pair, c, w, last_pair=False):
                if c == 0:
                    pe.wait_ge(olo_done, pair + 1)
                pe.wait_ge(otlo_done, 8 * pair + 5 + c)
                if c >= 2 or last_pair:
                    pe.wait_ge(wo_added, w - 1)
                else:
                    pe.wait_ge(v_copied, w + 7)
                for i in range(2):
                    t = 2 * c + i
                    n = 0
                    for a in range(2):
                        for ot, wt in ((oT_hi(a), o_lo), (oT_lo(a), o_hi), (oT_hi(a), o_hi)):
                            last = mm(VO[c % 2][:, i * 256:(i + 1) * 256], ot[:, t * P:(t + 1) * P], wt[:, a],
                                      start=(n == 0), stop=(n == 5))
                            n += 1
                last.then_inc(wo_done, 1)

            def means_of_abs(n):
                pe.wait_ge(abs_done, 8)
                pe.wait_ge(proj_copied, n + 4)
                mm(PR[0][:, 0:8], mean_ones[:], abs_sum[:].rearrange("p k i -> p (k i)"),
                   start=True, stop=True).then_inc(mean_done, 1)

            def pair_steps(pair, first, last):
                for s in range(LAST_STEPS if last else 8):
                    n = 8 * pair + s
                    a, j = s // 4, s % 4
                    pa, pj = before(s)
                    if not (first and s == 0):
                        transpose_probs(n - 1, pj)
                    if last and s == 2:
                        pe.wait_ge(mean_read, 2)
                    project(2 * pair + a + 1, 1 - a, j, n + 4)
                    if last and s == 1:
                        means_of_abs(n)
                    if 1 <= s <= 4 and not first:
                        project_out(pair - 1, s - 1, 4 * pair - 5 + s)
                    if first and s == 0:
                        project_v(0, 2, 2)
                    if first and s == 3:
                        project_v(0, 3, 3)
                    if s == 0 and not first:
                        project_v(pair, 3, 4 * pair + 3)
                    if s >= 5 and not last:
                        project_v(pair + 1, s - 5, 4 * pair + s - 1)
                    if s % 2 == 0:
                        scores(n + 1, 2 * pair + (s + 1) // 4, (s + 1) // 4 % 2, (s + 1) % 4)
                    if not (first and s == 0):
                        weigh_v(n - 1, pair if s > 0 else pair - 1, pa, pj)
                    if s % 2 == 1:
                        scores(n + 1, 2 * pair + (s + 1) // 4, (s + 1) // 4 % 2, (s + 1) % 4)

            pe.wait_ge(consts_set, 1)
            keep_warm(VO[0], 13)
            pe.wait_ge(ident_in, 16)
            transpose_x(0, 0)
            keep_warm(VO[0], 7)
            project(0, 0, 0, 0, 0)
            project(0, 0, 1, 1)
            transpose_x(0, 1)
            project_v(0, 0, 0)
            project(0, 0, 2, 2, KD)
            project(0, 0, 3, 3)
            project_v(0, 1, 1)
            scores(0, 0, 0, 0)
            pair_steps(0, True, False)
            with pe.Fori(1, PAIRS - 1) as pair:
                pair_steps(pair, False, False)
            pair_steps(PAIRS - 1, False, True)
            transpose_probs(LAST - 4, 3)
            project_out(PAIRS - 2, 3, 4 * PAIRS - 5)
            scores(LAST - 2, 2 * PAIRS - 1, 1, 1)
            weigh_v(LAST - 4, PAIRS - 1, 0, 3)
            transpose_probs(LAST - 3, 0)
            pe.wait_ge(proj_copied, CHUNKS)
            keep_warm(PR[1], 4)
            scores(LAST - 1, 2 * PAIRS - 1, 1, 2)
            weigh_v(LAST - 3, PAIRS - 1, 1, 0)
            transpose_probs(LAST - 2, 1)
            scores(LAST, 2 * PAIRS - 1, 1, 3)
            project_out(PAIRS - 1, 0, 4 * PAIRS - 4, True)
            weigh_v(LAST - 2, PAIRS - 1, 1, 1)
            transpose_probs(LAST - 1, 2)
            project_out(PAIRS - 1, 1, 4 * PAIRS - 3, True)
            weigh_v(LAST - 1, PAIRS - 1, 1, 2)
            transpose_probs(LAST, 3)
            project_out(PAIRS - 1, 2, 4 * PAIRS - 2, True)
            weigh_v(LAST, PAIRS - 1, 1, 3)
            transpose_x(1, 0)
            project_out(PAIRS - 1, 3, 4 * PAIRS - 1)

            hb = [SC[0], SC[1], VO[0], VO[1]]
            for half in range(2):
                for f in range(NF):
                    k = half * NF + f
                    if k == 0:
                        pe.wait_ge(tern_done[0], 1)
                    if k == NF // 2:
                        pe.wait_ge(tern_done[2], KD)
                    if k in (2, 3):
                        pe.wait_ge(wo_added, 4 * PAIRS - 3 + k)
                    if k >= 4:
                        pe.wait_ge(gelu_done, k - 3)
                    for kd in range(KD):
                        if f == 0:
                            pe.wait_ge(xt_lo_done, (2 + half) * KD + kd + 1)
                        for p_, xt in enumerate((xT_lo, xT_hi)):
                            last = mm(hb[k % 4][:], w1_sb[:, kd, f * P:(f + 1) * P],
                                      xt[:, kd, half * HALF:(half + 1) * HALF],
                                      start=(kd == 0 and p_ == 0), stop=(kd == KD - 1 and p_ == 1))
                    last.then_inc(h_done, 1)
                    if k == 4:
                        transpose_x(1, 1)
            yb = [OT, PT, PR[0], PR[1], SC[0]]
            pe.wait_ge(tern_done[1], 1)
            for c in range(NT // 2):
                pe.wait_ge(glo_done[0], (c // 2 + 1) * NF // 2)
                pe.wait_ge(glo_done[1], (c // 2 + 1) * NF // 2)
                for i in range(2):
                    t = 2 * c + i
                    for f in range(NF):
                        for p_, gt in enumerate((gT_lo, gT_hi)):
                            last = mm(yb[4 if t == NT - 1 else c][:, i * 256:(i + 1) * 256], gt[:, f, t * P:(t + 1) * P],
                                      w2_sb[:, f], start=(f == 0 and p_ == 0), stop=(f == NF - 1 and p_ == 1))
                    if i == 1 or c == NT // 2 - 1:
                        last.then_inc(y_done, 1)

        @block.scalar
        def _(act):
            copy = nc.scalar.copy

            def xt_hi(ln, half):
                banks = (SC, PR)[ln]
                for kd in range(KD):
                    act.wait_ge(xt_ready, ln * 4 + half * 2 + kd + 1)
                    copy(xT_hi[:, kd, half * HALF:(half + 1) * HALF], banks[kd][:]).then_inc(xt_hi_done, 1)

            def qkhi(a, loads, head, reused):
                act.wait_ge(qk_in[a], 32 * loads)
                if reused:
                    act.wait_ge(proj_done, 4 * (head - 1))
                copy(qk_hi[a][:], qk_raw[a][:]).then_inc(qkhi_done, 1)

            def vhi(pair, reused):
                act.wait_ge(v_in, 16 * (pair + 1))
                if reused:
                    act.wait_ge(v_done, 4 * pair)
                copy(v_hi[:], v_raw[:]).then_inc(vhi_done, 1)

            def ohi(pair, reused):
                act.wait_ge(o_in, 16 * (pair + 1))
                if reused:
                    act.wait_ge(wo_done, 4 * pair)
                copy(o_hi[:], o_raw[:]).then_inc(ohi_done, 1)

            def copy_proj(c, m):
                act.wait_ge(proj_done, m + 1)
                if not (isinstance(m, int) and m < 4):
                    act.wait_ge(rotlo_done, m - 3)
                copy(turn[c][:], PR[c % 2][:]).then_inc(proj_copied, 1)

            def rothi(a, c, m):
                act.wait_ge(rot_done, m + 1)
                copy(rot_hi(a, c % 2)[:, half_of(c)], turn[c][:]).then_inc(rothi_done, 1)

            def exps(n, j):
                act.wait_ge(negmax_done, n + 1)
                for i in range(2):
                    nc.scalar.activation(probs[j % 2][:, i], SC[j % 2][:, i * 256 + P:(i + 1) * 256], ACT.Exp,
                                         bias=negmax[:, j % 2, i:i + 1], scale=SCALE,
                                         accum_out=rowsum[:, j % 2, i:i + 1]).then_inc(exp_done, 1)

            def scale_probs(n, j):
                act.wait_ge(rinv_done, n + 1)
                for i in range(2):
                    last = nc.scalar.activation(probs[j % 2][:, i], probs[j % 2][:, i], ACT.Copy,
                                                scale=rinv[:, j % 2, i:i + 1])
                last.then_inc(scaled, 1)

            def copy_v(c, v):
                act.wait_ge(v_done, v + 1)
                copy(v_sb[:, 2 * c:2 * c + 2], VO[c % 2][:].rearrange("p (t n) -> p t n", t=2)).then_inc(v_copied, 1)

            def ot_hi(n, a, j):
                act.wait_ge(pv_done, n + 1)
                copy(oT_hi(a)[:, 2 * j * P:(2 * j + 2) * P], OT[:, 0:256]).then_inc(othi_done, 1)

            def abs_sums(k, i):
                act.wait_ge(w12_in[k], 16 * (k + 1))
                raw = (w1_raw, w2_raw)[k]
                dest = (w1_sb, w2_sb)[k][:].rearrange("p a b -> p (a b)")
                cs = slice(i * NW // P // 4, (i + 1) * NW // P // 4)
                nc.scalar.activation(dest[:, cs], raw[:, cs], ACT.Abs,
                                     accum_out=abs_sum[:, k, i:i + 1]).then_inc(abs_done, 1)

            def pair_steps(pair, first, last):
                for s in range(LAST_STEPS if last else 8):
                    n = 8 * pair + s
                    m = n + 4
                    a, j = s // 4, s % 4
                    if not (first and s == 0):
                        a2, c2 = before(s + 4, 2)
                        rothi(a2, c2, m - 2)
                    in_haste = (first and s == 0) or (last and s == 3)
                    if in_haste:
                        copy_proj(j, m)
                    exps(n, j)
                    if first and s == 0:
                        scale_probs(n, j)
                        rothi(0, 2, 2)
                    if not in_haste:
                        copy_proj(j, m)
                    if not (first and s == 0):
                        scale_probs(n, j)
                        ot_hi(n - 1, *before(s))
                    if s == 0 and not first:
                        copy_v(2, 4 * pair + 2)
                    if s == 1 and not first:
                        copy_v(3, 4 * pair + 3)
                    if s == 0 and first:
                        copy_v(2, 2)
                    if s == 3 and first:
                        copy_v(3, 3)
                    if s >= 6 and not last:
                        copy_v(s - 6, 4 * pair + s - 2)
                    if s == 1 and not last:
                        qkhi(0, pair + 2, 2 * pair + 2, True)
                    if s == 5 and not last:
                        qkhi(1, pair + 2, 2 * pair + 3, True)
                    if s == 3 and not last:
                        vhi(pair + 1, True)
                    if s == 6:
                        ohi(pair, not first)
                    if first and s > 0:
                        abs_sums((s - 1) // 4, (s - 1) % 4)

            nc.scalar.preload_act_table(ACT.Exp)
            qkhi(0, 1, 0, False)
            vhi(0, False)
            xt_hi(0, 0)
            qkhi(1, 1, 1, False)
            copy_proj(0, 0)
            copy_proj(1, 1)
            xt_hi(0, 1)
            copy_v(0, 0)
            rothi(0, 0, 0)
            copy_proj(2, 2)
            rothi(0, 1, 1)
            copy_proj(3, 3)
            copy_v(1, 1)
            pair_steps(0, True, False)
            abs_sums(1, 3)
            with act.Fori(1, PAIRS - 1) as pair:
                pair_steps(pair, False, False)
            pair_steps(PAIRS - 1, False, True)
            rothi(1, 2, CHUNKS - 2)
            exps(LAST - 3, 0)
            ohi(PAIRS - 1, True)
            scale_probs(LAST - 3, 0)
            rothi(1, 3, CHUNKS - 1)
            ot_hi(LAST - 4, 0, 3)
            exps(LAST - 2, 1)
            scale_probs(LAST - 2, 1)
            ot_hi(LAST - 3, 1, 0)
            exps(LAST - 1, 2)
            scale_probs(LAST - 1, 2)
            exps(LAST, 3)
            ot_hi(LAST - 2, 1, 1)
            scale_probs(LAST, 3)
            ot_hi(LAST - 1, 1, 2)
            nc.scalar.preload_act_table(ACT.Gelu)
            ot_hi(LAST, 1, 3)
            xt_hi(1, 0)
            act.wait_ge(bias_in, 32)
            hb = [SC[0], SC[1], VO[0], VO[1]]
            for k in range(2 * NF):
                f = k % NF
                act.wait_ge(h_done, k + 1)
                if k >= 4:
                    by, count = lo_by(k - 4)
                    act.wait_ge(glo_done[by], count)
                nc.scalar.activation(gelu_tmp[k % 4][:], hb[k % 4][:], ACT.Gelu,
                                     bias=b1_sb[:, f:f + 1]).then_inc(gelu_done, 1)
                if k % 4 == 3:
                    hs = slice((k // NF) * HALF, (k // NF + 1) * HALF)
                    act.wait_ge(gelu_done, k + 1)
                    copy(gT_hi[:, f, hs], gelu_tmp[k % 4][:]).then_inc(ghi_done[1], 1)
                if k == 4:
                    xt_hi(1, 1)

        @block.vector
        def _(dve):
            tt = nc.vector.tensor_tensor

            def tile_stats(ln, pair):
                if ln == 0:
                    dve.wait_ge(x_in[pair], 16)
                else:
                    dve.wait_ge(wo_added, 4 * PAIRS - 3 + pair)
                for t in range(2 * pair, 2 * pair + 2):
                    nc.vector.bn_stats(stats[:, t], xres[:, t]).then_inc(bn_done, 1)

            def moments(ln, half):
                hs = slice(half * 4, half * 4 + 4)
                for t in range(half * 4, half * 4 + 4):
                    dve.wait_ge(bn_done, ln * NT + t + 1)
                    nc.vector.bn_aggr(mv[:, t], stats[:, t]).then_inc(aggr_done, 1)
                dve.wait_ge(aggr_done, ln * NT + half * 4 + 4)
                nc.vector.tensor_scalar(var_eps[:, hs], mv[:, hs, 1], EPS_LN, None, ALU.add).then_inc(var_ready, 1)

            def normalise(ln, half):
                dve.wait_ge(rstd_ready, 2 * ln + half + 1)
                for t in range(half * 4, half * 4 + 4):
                    nc.vector.tensor_scalar(xnorm[:, t], xres[:, t], mv[:, t, 0:1], rstd[:, t:t + 1],
                                            ALU.subtract, ALU.mult).then_inc(xn_ready, 1)

            def xt_lo(ln, half):
                banks = (SC, PR)[ln]
                hs = slice(half * HALF, (half + 1) * HALF)
                for kd in range(KD):
                    dve.wait_ge(xt_hi_done, ln * 4 + half * 2 + kd + 1)
                    tt(xT_lo[:, kd, hs], banks[kd][:], xT_hi[:, kd, hs].bitcast(F32),
                       ALU.subtract).then_inc(xt_lo_done, 1)

            def times_cos(c, m, swaps):
                dve.wait_ge(swap_in[c], 32 * swaps)
                tt(turn[c][:], turn[c][:], cos_sb[:, half_of(c)], ALU.mult).then_inc(cos_done, 1)

            def early_cos(c):
                if c == 0:
                    dve.wait_ge(tab_in[0], 32)
                dve.wait_ge(proj_copied, c + 1)
                tt(cos_product[:, c * HALF:(c + 1) * HALF], turn[c][:], cos_sb[:, half_of(c)],
                   ALU.mult).then_inc(cos_done, 1)

            def rotate_sin(c, m, swaps):
                dve.wait_ge(swap_in[c], 32 * swaps)
                if m > 0:
                    dve.wait_ge(sin_done, m)
                tt(swapped[c][:], swapped[c][:], sin_sb[:, half_of(c)], ALU.mult).then_inc(sin_done, 1)

            def rotate_add(c, m, product):
                if m > 0:
                    dve.wait_ge(rot_done, m)
                dve.wait_ge(cos_done, m + 1)
                dve.wait_ge(sin_done, m + 1)
                tt(turn[c][:], product, swapped[c][:], ALU.add).then_inc(rot_done, 1)

            def rotlo(a, c, m):
                dve.wait_ge(rothi_done, m + 1)
                tt(rot_lo(a, c % 2)[:, half_of(c)], turn[c][:], rot_hi(a, c % 2)[:, half_of(c)].bitcast(F32),
                   ALU.subtract).then_inc(rotlo_done, 1)

            def merge(n, j, first_in_loop):
                if first_in_loop:
                    dve.wait_ge(scores_done, n + 1)
                    nc.vector.memset(rowsum[:, j % 2], 0.0)
                else:
                    dve.wait_ge(mask_in, 32)
                    dve.wait_ge(scores_done, n + 1)
                sc = SC[j % 2][:].rearrange("p (i b k) -> p i b k", i=2, b=2)
                if j == 0:
                    nc.vector.copy_predicated(sc[:, 0, 1], in_prev_sb[:], nothing[:])
                    nc.vector.copy_predicated(sc[:, 1, 1], in_prev_sb[:], sc[:, 1, 0]).then_inc(merged, 1)
                else:
                    nc.vector.copy_predicated(sc[:, :, 1], in_prev_sb[:].unsqueeze(1).broadcast_to([P, 2, P]),
                                              sc[:, :, 0]).then_inc(merged, 1)
                dve.wait_ge(merged, n + 1)
                nc.vector.tensor_reduce(rowmax[:, j % 2], sc[:, :, 1], AX.X, ALU.max).then_inc(max_done, 1)
                dve.wait_ge(max_done, n + 1)
                nc.vector.tensor_scalar(negmax[:, j % 2], rowmax[:, j % 2], -SCALE, None,
                                        ALU.mult).then_inc(negmax_done, 1)

            def inverse_sum(n, j):
                dve.wait_ge(exp_done, 2 * n + 2)
                nc.vector.reciprocal(rinv[:, j % 2], rowsum[:, j % 2]).then_inc(rinv_done, 1)

            def mask_pt(n):
                dve.wait_ge(pt_done, n + 1)
                if not (isinstance(n, int) and n == 0):
                    dve.wait_ge(pv_done, n)
                tt(probsT[:], PT[:, 0:256].rearrange("p (i q) -> p i q", i=2).unsqueeze(2).broadcast_to([P, 2, 2, P]),
                   mask_sb[:].unsqueeze(1).broadcast_to([P, 2, 2, P]), ALU.mult).then_inc(pt_masked, 1)

            def ot_lo(n, a, j):
                dve.wait_ge(othi_done, n + 1)
                ts = slice(2 * j * P, (2 * j + 2) * P)
                tt(oT_lo(a)[:, ts], OT[:, 0:256], oT_hi(a)[:, ts].bitcast(F32), ALU.subtract).then_inc(otlo_done, 1)

            def add_out(c, w):
                dve.wait_ge(wo_done, w + 1)
                ts = slice(2 * c, 2 * c + 2)
                tt(xres[:, ts], VO[c % 2][:].rearrange("p (t d) -> p t d", t=2), xres[:, ts], ALU.add).then_inc(wo_added, 1)

            def thresholds():
                dve.wait_ge(mean_done, 1)
                for k in range(2):
                    nc.vector.tensor_reduce(mean_abs[:, k:k + 1], PR[0][:, 4 * k:4 * k + 4], AX.X,
                                            ALU.add).then_inc(mean_read, 1)
                dve.wait_ge(mean_read, 2)
                nc.vector.tensor_scalar(thr[:, :, 0], mean_abs[:], EPS_Q, 0.5, ALU.max, ALU.mult)
                nc.vector.tensor_scalar(thr[:, :, 1], mean_abs[:], EPS_Q, -0.5, ALU.max, ALU.mult).then_inc(thr_done, 1)

            def below_w1():
                raw = w1_raw[:].rearrange("p (k f) -> p k f", k=KD)
                dve.wait_ge(thr_done, 1)
                nc.vector.tensor_scalar(w1_sb[:, :, F // 2:], raw[:, :, F // 2:], thr[:, 0, 1:2], None,
                                        ALU.is_lt).then_inc(below_done[2], 1)

            def ternary_w1(kd):
                raw = w1_raw[:].rearrange("p (k f) -> p k f", k=KD)[:, kd, F // 2:]
                dest = w1_sb[:, kd, F // 2:]
                dve.wait_ge(below_done[2], 1)
                nc.vector.scalar_tensor_tensor(dest, raw, thr[:, 0, 0:1], dest.bitcast(F32), ALU.is_gt,
                                               ALU.subtract).then_inc(tern_done[2], 1)

            def ternary_w2():
                dest = w2_sb[:].rearrange("p a b -> p (a b)")
                dve.wait_ge(below_done[1], 1)
                nc.vector.scalar_tensor_tensor(dest, w2_raw[:], thr[:, 1, 0:1], dest.bitcast(F32), ALU.is_gt,
                                               ALU.subtract).then_inc(tern_done[1], 1)

            def pair_steps(pair, first, last):
                for s in range(LAST_STEPS if last else 8):
                    n = 8 * pair + s
                    m = n + 4
                    j = s % 4
                    merge(n, j, s < 2 and not isinstance(n, int))
                    if first and s == 1:
                        rotate_add(3, 3, turn[3][:])
                    c1 = (s - 1) % 4
                    in_haste = last and s == 3
                    if not (first and s == 0):
                        mask_pt(n - 1)
                    if in_haste:
                        times_cos(c1, m - 1, 2 * pair + (s + 3) // 4 + 1)
                    if first and s == 0:
                        times_cos(2, 2, 1)
                        times_cos(3, 3, 1)
                        inverse_sum(n, j)
                        rotate_sin(3, 3, 1)
                    else:
                        if first and s == 1:
                            dve.wait_ge(rotlo_done, 3)
                        rotlo(*before(s + 4, 2), m - 2)
                        inverse_sum(n, j)
                    if not (first and s == 0) and not in_haste:
                        times_cos(c1, m - 1, 2 * pair + (s + 3) // 4 + 1)
                    if 1 <= s <= 4 and not first:
                        add_out(s - 1, 4 * pair - 5 + s)
                    if last and s == 1:
                        thresholds()
                    if not (first and s == 0):
                        ot_lo(n - 1, *before(s))
                    if last and s == 1:
                        below_w1()

            nc.vector.memset(mean_ones[:], 1.0 / NW)
            nc.vector.memset(minus_half[:], -0.5).then_inc(consts_set, 1)
            tile_stats(0, 0)
            tile_stats(0, 1)
            moments(0, 0)
            tile_stats(0, 2)
            normalise(0, 0)
            tile_stats(0, 3)
            moments(0, 1)
            xt_lo(0, 0)
            normalise(0, 1)
            early_cos(0)
            early_cos(1)
            xt_lo(0, 1)
            for c in range(2):
                rotate_sin(c, c, 1)
                rotate_add(c, c, cos_product[:, c * HALF:(c + 1) * HALF])
            rotlo(0, 0, 0)
            rotlo(0, 1, 1)
            dve.wait_ge(tab_in[1], 32)
            dve.wait_ge(nothing_set, 1)
            dve.wait_ge(mask_in, 32)
            pair_steps(0, True, False)
            with dve.Fori(1, PAIRS - 1) as pair:
                pair_steps(pair, False, False)
            pair_steps(PAIRS - 1, False, True)
            merge(LAST - 3, 0, False)
            mask_pt(LAST - 4)
            rotate_sin(3, CHUNKS - 1, 2 * PAIRS)
            inverse_sum(LAST - 3, 0)
            rotate_add(3, CHUNKS - 1, turn[0][:])
            merge(LAST - 2, 1, False)
            rotlo(1, 3, CHUNKS - 1)
            ot_lo(LAST - 4, 0, 3)
            mask_pt(LAST - 3)
            inverse_sum(LAST - 2, 1)
            merge(LAST - 1, 2, False)
            ot_lo(LAST - 3, 1, 0)
            mask_pt(LAST - 2)
            inverse_sum(LAST - 1, 2)
            merge(LAST, 3, False)
            add_out(3, 4 * PAIRS - 5)
            ternary_w1(0)
            ot_lo(LAST - 2, 1, 1)
            mask_pt(LAST - 1)
            inverse_sum(LAST, 3)
            add_out(0, 4 * PAIRS - 4)
            tile_stats(1, 0)
            add_out(1, 4 * PAIRS - 3)
            ot_lo(LAST - 1, 1, 2)
            tile_stats(1, 1)
            moments(1, 0)
            mask_pt(LAST)
            ternary_w1(1)
            normalise(1, 0)
            ot_lo(LAST, 1, 3)
            add_out(2, 4 * PAIRS - 2)
            xt_lo(1, 0)
            tile_stats(1, 2)
            add_out(3, 4 * PAIRS - 1)
            tile_stats(1, 3)
            moments(1, 1)

            def ghi(k):
                hs = slice((k // NF) * HALF, (k // NF + 1) * HALF)
                dve.wait_ge(gelu_done, k + 1)
                nc.vector.tensor_copy(gT_hi[:, k % NF, hs], gelu_tmp[k % 4][:]).then_inc(ghi_done[0], 1)

            def glo(k):
                hs = slice((k // NF) * HALF, (k // NF + 1) * HALF)
                by, count = hi_by(k)
                dve.wait_ge(ghi_done[by], count)
                tt(gT_lo[:, k % NF, hs], gelu_tmp[k % 4][:], gT_hi[:, k % NF, hs].bitcast(F32),
                   ALU.subtract).then_inc(glo_done[0], 1)

            ghi(0)
            glo(0)
            normalise(1, 1)
            for k in range(2 * NF):
                if (k + 1) % 4 != 3 and k + 1 < 2 * NF:
                    ghi(k + 1)
                if k % 2 == 0 and k > 0:
                    glo(k)
                if k == 3:
                    xt_lo(1, 1)
                if k == 8:
                    ternary_w2()
            yb = [OT, PT, PR[0]]
            dve.wait_ge(b2_added, NT)
            for c in range(NT // 2 - 1):
                dve.wait_ge(y_done, c + 1)
                tt(final[:, 2 * c:2 * c + 2], yb[c][:].rearrange("p (t d) -> p t d", t=2), xres[:, 2 * c:2 * c + 2],
                   ALU.add).then_inc(fin_done, 1)
            for t in (NT - 2, NT - 1):
                y = PR[1][:, 0:256] if t == NT - 2 else SC[0][:, 256:512]
                dve.wait_ge(y_done, t - NT // 2 + 2)
                tt(final[:, t], y, xres[:, t], ALU.add).then_inc(fin_done, 1)

        @block.gpsimd
        def _(pool):
            tt = nc.gpsimd.tensor_tensor

            def rsqrt(ln, half):
                hs = slice(half * 4, half * 4 + 4)
                pool.wait_ge(var_ready, 2 * ln + half + 1)
                tt(rstd[:, hs], var_eps[:, hs], minus_half[:, hs], ALU.pow).then_inc(rstd_ready, 1)

            def qklo(a, head):
                pool.wait_ge(qkhi_done, head + 1)
                tt(qk_lo[a][:], qk_raw[a][:], qk_hi[a][:].bitcast(F32), ALU.subtract).then_inc(qklo_done, 1)

            def vlo(pair):
                pool.wait_ge(vhi_done, pair + 1)
                tt(v_lo[:], v_raw[:], v_hi[:].bitcast(F32), ALU.subtract).then_inc(vlo_done, 1)

            def olo(pair):
                pool.wait_ge(ohi_done, pair + 1)
                tt(o_lo[:], o_raw[:], o_hi[:].bitcast(F32), ALU.subtract).then_inc(olo_done, 1)

            def rotate(c, m, swaps):
                pool.wait_ge(swap_in[c], 32 * swaps)
                tt(swapped[c][:], swapped[c][:], sin_sb[:, half_of(c)], ALU.mult).then_inc(sin_done, 1)
                pool.wait_ge(cos_done, m + 1)
                pool.wait_ge(sin_done, m + 1)
                tt(turn[c][:], turn[c][:], swapped[c][:], ALU.add).then_inc(rot_done, 1)

            def ternary_w1(step):
                raw = w1_raw[:].rearrange("p (k f) -> p k f", k=KD)[:, :, :F // 2]
                dest = w1_sb[:, :, :F // 2]
                kd = step % KD
                if step == 0:
                    pool.wait_ge(thr_done, 1)
                if step < KD:
                    nc.gpsimd.tensor_scalar(dest[:, kd], raw[:, kd], thr[:, 0, 1:2], None,
                                            ALU.is_lt).then_inc(below_done[0], 1)
                elif step < 2 * KD:
                    nc.gpsimd.tensor_scalar(raw[:, kd], raw[:, kd], thr[:, 0, 0:1], None,
                                            ALU.is_gt).then_inc(above_done, 1)
                else:
                    pool.wait_ge(below_done[0], KD)
                    pool.wait_ge(above_done, KD)
                    tt(dest, raw, dest.bitcast(F32), ALU.subtract).then_inc(tern_done[0], 1)

            def below_w2():
                dest = w2_sb[:].rearrange("p a b -> p (a b)")
                nc.gpsimd.tensor_scalar(dest, w2_raw[:], thr[:, 1, 1:2], None, ALU.is_lt).then_inc(below_done[1], 1)

            def pair_steps(pair, first, last):
                for s in range(LAST_STEPS if last else 8):
                    m = 8 * pair + s + 4
                    if first and s == 0:
                        pool.wait_ge(rothi_done, 3)
                        tt(rot_lo(0, 0)[:, half_of(2)], turn[2][:], rot_hi(0, 0)[:, half_of(2)].bitcast(F32),
                           ALU.subtract).then_inc(rotlo_done, 1)
                    if first and s == 1:
                        pool.wait_ge(rot_done, 4)
                    if not (first and s == 0):
                        rotate((s - 1) % 4, m - 1, 2 * pair + (s + 3) // 4 + 1)
                    if s == 1 and not last:
                        qklo(0, 2 * pair + 2)
                    if s == 5 and not last:
                        qklo(1, 2 * pair + 3)
                    if s == 3 and not last:
                        vlo(pair + 1)
                    if s == 6:
                        olo(pair)

            nc.gpsimd.memset(nothing[:], -BIG).then_inc(nothing_set, 1)
            pool.wait_ge(consts_set, 1)
            rsqrt(0, 0)
            qklo(0, 0)
            rsqrt(0, 1)
            vlo(0)
            qklo(1, 1)
            pool.wait_ge(tab_in[1], 32)
            pool.wait_ge(rot_done, 2)
            rotate(2, 2, 1)
            pair_steps(0, True, False)
            with pool.Fori(1, PAIRS - 1) as pair:
                pair_steps(pair, False, False)
            pair_steps(PAIRS - 1, False, True)
            pool.wait_ge(proj_copied, CHUNKS)
            pool.wait_ge(rotlo_done, CHUNKS - 3)
            tt(turn[0][:], turn[3][:], cos_sb[:, half_of(3)], ALU.mult).then_inc(cos_done, 1)
            pool.wait_ge(rothi_done, CHUNKS - 1)
            tt(rot_lo(1, 0)[:, half_of(2)], turn[2][:], rot_hi(1, 0)[:, half_of(2)].bitcast(F32),
               ALU.subtract).then_inc(rotlo_done, 1)
            olo(PAIRS - 1)
            for step in range(2 * KD + 1):
                ternary_w1(step)
            rsqrt(1, 0)
            below_w2()
            rsqrt(1, 1)
            pool.wait_ge(bias_in, 32)
            for k in range(2 * NF):
                hs = slice((k // NF) * HALF, (k // NF + 1) * HALF)
                if k % 2 == 1:
                    by, count = hi_by(k)
                    pool.wait_ge(ghi_done[by], count)
                    tt(gT_lo[:, k % NF, hs], gelu_tmp[k % 4][:], gT_hi[:, k % NF, hs].bitcast(F32),
                       ALU.subtract).then_inc(glo_done[1], 1)
                if k % 2 == 0:
                    t = k // 2
                    pool.wait_ge(xn_ready, NT + t + 1)
                    tt(xres[:, t], xres[:, t], b2_sb[:], ALU.add).then_inc(b2_added, 1)


def tables(T, HD):
    import numpy as np
    inv_freq = (np.float32(1.0) / np.power(np.float32(10000.0), np.arange(0, HD, 2, dtype=np.float32) / np.float32(HD))).astype(np.float32)
    freqs = np.arange(T, dtype=np.float32)[:, None] * inv_freq[None, :]
    c, s = np.cos(freqs).astype(np.float32).T, np.sin(freqs).astype(np.float32).T
    q = np.arange(HD)[:, None]
    k = np.arange(HD)[None, :]
    prev = k > q
    mask_t = np.concatenate([prev.T, ~prev.T], 1)
    return {"cos_t": np.concatenate([c, c], 0), "sin_t": np.concatenate([-s, s], 0),
            "in_prev": prev.astype(np.int32), "mask_t": mask_t.astype(np.float32), "ident": np.eye(HD, dtype=np.float32)}


def kernel(L0_attn_hidden_states, L0_attn_wq, L0_attn_wk, L0_attn_wv, L0_attn_wo, L0_ffn_w1, L0_ffn_b1, L0_ffn_w2,
           L0_ffn_b2):
    import numpy as np
    import concourse.bacc as bacc
    from concourse.bass_utils import run_bass_kernel_spmd as run

    x = np.asarray(L0_attn_hidden_states)
    arrays = {"x": x[0], "wq": L0_attn_wq, "wk": L0_attn_wk, "wv": L0_attn_wv, "wo": L0_attn_wo,
              "w1t": np.asarray(L0_ffn_w1).T, "b1": np.asarray(L0_ffn_b1).reshape(-1, P).T, "w2t": np.asarray(L0_ffn_w2).T, "b2": L0_ffn_b2,
              **tables(x.shape[1], P)}
    arrays = {k: np.ascontiguousarray(v) for k, v in arrays.items()}
    nc = bacc.Bacc("TRN2", target_bir_lowering=False, num_devices=1)
    args = {k: nc.dram_tensor(f"in_{k}", v.shape, mybir.dt.from_np(v.dtype), kind="ExternalInput").ap()
            for k, v in arrays.items()}
    out = nc.dram_tensor("out_y", x[0].shape, F32, kind="ExternalOutput").ap()
    preln_block_kernel(nc, out=out, **args)
    r = run(nc, [{f"in_{k}": v for k, v in arrays.items()}], core_ids=[0])
    return r.results[0]["out_y"].reshape(x.shape)
```
